# Optimizing a Trainium2 kernel written in Bass

```python
import numpy as np
import jax
import jax.numpy as jnp

def _softmax(x, axis=-1):
    return jax.nn.softmax(x, axis=axis)

def _gelu(x):
    return jax.nn.gelu(x, approximate=True)

def _silu(x):
    return jax.nn.silu(x)

def _sigmoid(x):
    return jax.nn.sigmoid(x)

def _layernorm(x, axis=-1, eps=1e-05):
    m = jnp.mean(x, axis=axis, keepdims=True)
    v = jnp.var(x, axis=axis, keepdims=True)
    return (x - m) / jnp.sqrt(v + eps)

def _scatter_add(tgt, idx, src, axis=0):
    return tgt.at[idx].add(src)

def _segment_sum(src, seg, n):
    return jax.ops.segment_sum(src, seg, n)
kernel_name = 'mk_xattn_ffn_d2_seqx_r4_24dd04'

def setup_inputs(seed: int=0):
    np.random.seed(seed)
    _w = jnp.asarray

    def _rec_inputs():
        import jax
        import jax.numpy as jnp
        _rk = jax.random.key(seed)
        x = 7.22e-05 + 1 * jax.random.normal(jax.random.fold_in(_rk, 1), (16, 256, 256), jnp.float32)
        _lenS = 256 - jax.random.randint(jax.random.fold_in(_rk, 7), (16,), 0, max(1, 256 // 4) + 1, jnp.int32)
        _lenS2 = 120 - jax.random.randint(jax.random.fold_in(_rk, 8), (16,), 0, max(1, 120 // 4) + 1, jnp.int32)
        _ctx_1024P = jax.random.normal(jax.random.fold_in(_rk, 11), (16, 16, 256), jnp.float32)
        _ctx_1024c = jax.random.dirichlet(jax.random.fold_in(_rk, 511), 0.3 * jnp.ones((16,), jnp.float32), (16, 120))
        _ctx_1024t = jnp.einsum('bsk,bkd->bsd', _ctx_1024c, _ctx_1024P)
        _ctx_1024t = _ctx_1024t * jax.lax.rsqrt(jnp.mean(jnp.square(_ctx_1024t)) + 1e-12) * 0.953939
        ctx_1024 = -1.39393e-06 + 0.999914 * (_ctx_1024t + 0.3 * jax.random.normal(jax.random.fold_in(_rk, 611), (16, 120, 256), jnp.float32))
        fside_BxSxS2_0 = -1.47943e-05 + 1.00017 * jax.random.normal(jax.random.fold_in(_rk, 13), (16, 256, 120), jnp.float32)
        _validS = jnp.arange(256)[None, :] < _lenS[:, None]
        _validS2 = jnp.arange(120)[None, :] < _lenS2[:, None]
        _causal = jnp.tril(jnp.ones((256, 256), dtype=bool))
        mask_BxS2_bf1 = jnp.ones((16, 120), dtype=bool)
        return (x, ctx_1024, fside_BxSxS2_0, mask_BxS2_bf1)
    x, ctx_1024, fside_BxSxS2_0, mask_BxS2_bf1 = _rec_inputs()

    def _L0_xattn_setup():
        import jax, jax.numpy as jnp
        import numpy as np
        HEADS = 16
        DIM_HEAD = 64
        SCALE = DIM_HEAD ** (-0.5)
        key = jax.random.key(seed)
        ks = jax.random.split(key, 6)
        B, Nq, Nkv, D = (4, 512, 256, 256)
        inner = HEADS * DIM_HEAD
        return {'x': jax.random.normal(ks[0], (B, Nq, D), dtype=jnp.float32), 'context': jax.random.normal(ks[1], (B, Nkv, D), dtype=jnp.float32), 'mask': jnp.ones((B, Nkv), dtype=bool), 'Wq': jax.random.normal(ks[2], (inner, D), dtype=jnp.float32) * D ** (-0.5), 'Wkv': jax.random.normal(ks[3], (2 * inner, D), dtype=jnp.float32) * D ** (-0.5), 'Wout': jax.random.normal(ks[4], (D, inner), dtype=jnp.float32) * inner ** (-0.5), 'b_out': jnp.zeros((D,), dtype=jnp.float32)}
    _L0_xattn_all = _L0_xattn_setup()
    _L0_xattn_in = {k: v for k, v in _L0_xattn_all.items() if k in ('Wq', 'Wkv', 'Wout', 'b_out')}
    del _L0_xattn_all

    def _L0_ffn_setup():
        import jax, jax.numpy as jnp
        import numpy as np
        B, T, C, H, E = (4, 512, 256, 512, 8)
        CAPACITY_FACTOR = 1.0
        key = jax.random.key(seed)
        ks = jax.random.split(key, 5)
        scale = 0.02
        return {'x': jax.random.normal(ks[0], (B, T, C), dtype=jnp.float32), 'Wg': jax.random.normal(ks[1], (E, C), dtype=jnp.float32) * scale, 'W1': jax.random.normal(ks[2], (E, H, C), dtype=jnp.float32) * scale, 'W2': jax.random.normal(ks[3], (E, C, H), dtype=jnp.float32) * scale, 'W3': jax.random.normal(ks[4], (E, H, C), dtype=jnp.float32) * scale}
    _L0_ffn_all = _L0_ffn_setup()
    _L0_ffn_in = {k: v for k, v in _L0_ffn_all.items() if k in ('Wg', 'W1', 'W2', 'W3')}
    del _L0_ffn_all

    def _L1_xattn_setup():
        import jax, jax.numpy as jnp
        import numpy as np
        D = 256
        key = jax.random.key(seed)
        ks = jax.random.split(key, 13)
        B, S, d = (4, 512, D)
        inp = {'q_in': jax.random.normal(ks[0], (B, S, d), jnp.float32), 'k_in': jax.random.normal(ks[1], (B, S, d), jnp.float32), 'v_in': jax.random.normal(ks[2], (B, S, d), jnp.float32), 'phi_risk': jax.random.normal(ks[3], (B, S, S), jnp.float32), 'phi_prio': jax.random.normal(ks[4], (B, S, S), jnp.float32), 'phi_impl': jax.random.normal(ks[5], (B, S, S), jnp.float32), 'Wq': jax.random.normal(ks[6], (d, d), jnp.float32) / np.sqrt(d), 'bq': jax.random.normal(ks[7], (d,), jnp.float32) * 0.01, 'Wk': jax.random.normal(ks[8], (d, d), jnp.float32) / np.sqrt(d), 'bk': jax.random.normal(ks[9], (d,), jnp.float32) * 0.01, 'Wv': jax.random.normal(ks[10], (d, d), jnp.float32) / np.sqrt(d), 'bv': jax.random.normal(ks[11], (d,), jnp.float32) * 0.01, 'beta_risk': jnp.float32(0.1), 'beta_prio': jnp.float32(0.1), 'beta_impl': jnp.float32(0.1)}
        return inp
    _L1_xattn_all = _L1_xattn_setup()
    _L1_xattn_in = {k: v for k, v in _L1_xattn_all.items() if k in ('Wq', 'bq', 'Wk', 'bk', 'Wv', 'bv', 'beta_risk', 'beta_prio', 'beta_impl')}
    del _L1_xattn_all

    def _L1_ffn_setup():
        import jax, jax.numpy as jnp
        import numpy as np
        D_MODEL = 256
        key = jax.random.key(seed)
        k_x, k_w, k_a1, k_a2 = jax.random.split(key, 4)
        x = jax.random.normal(k_x, (4, 512, D_MODEL), dtype=jnp.float32)
        weight = jax.random.normal(k_w, (D_MODEL, D_MODEL), dtype=jnp.float32) * 0.02
        aux_weight1 = jax.random.normal(k_a1, (D_MODEL, D_MODEL), dtype=jnp.float32) * 0.02
        aux_weight2 = jax.random.normal(k_a2, (D_MODEL, D_MODEL), dtype=jnp.float32) * 0.02
        bias = jnp.zeros((D_MODEL,), dtype=jnp.float32)
        return {'x': x, 'weight': weight, 'aux_weight1': aux_weight1, 'aux_weight2': aux_weight2, 'bias': bias}
    _L1_ffn_all = _L1_ffn_setup()
    _L1_ffn_in = {k: v for k, v in _L1_ffn_all.items() if k in ('weight', 'aux_weight1', 'aux_weight2', 'bias')}
    del _L1_ffn_all
    return {'x': x, 'ctx_1024': ctx_1024, 'fside_BxSxS2_0': fside_BxSxS2_0, 'mask_BxS2_bf1': mask_BxS2_bf1, 'L0_xattn_Wq': _L0_xattn_in['Wq'], 'L0_xattn_Wkv': _L0_xattn_in['Wkv'], 'L0_xattn_Wout': _L0_xattn_in['Wout'], 'L0_xattn_b_out': _L0_xattn_in['b_out'], 'L0_ffn_Wg': _L0_ffn_in['Wg'], 'L0_ffn_W1': _L0_ffn_in['W1'], 'L0_ffn_W2': _L0_ffn_in['W2'], 'L0_ffn_W3': _L0_ffn_in['W3'], 'L1_xattn_Wq': _L1_xattn_in['Wq'], 'L1_xattn_bq': _L1_xattn_in['bq'], 'L1_xattn_Wk': _L1_xattn_in['Wk'], 'L1_xattn_bk': _L1_xattn_in['bk'], 'L1_xattn_Wv': _L1_xattn_in['Wv'], 'L1_xattn_bv': _L1_xattn_in['bv'], 'L1_xattn_beta_risk': _L1_xattn_in['beta_risk'], 'L1_xattn_beta_prio': _L1_xattn_in['beta_prio'], 'L1_xattn_beta_impl': _L1_xattn_in['beta_impl'], 'L1_ffn_weight': _L1_ffn_in['weight'], 'L1_ffn_aux_weight1': _L1_ffn_in['aux_weight1'], 'L1_ffn_aux_weight2': _L1_ffn_in['aux_weight2'], 'L1_ffn_bias': _L1_ffn_in['bias']}

def reference(x, ctx_1024, fside_BxSxS2_0, mask_BxS2_bf1, L0_xattn_Wq, L0_xattn_Wkv, L0_xattn_Wout, L0_xattn_b_out, L0_ffn_Wg, L0_ffn_W1, L0_ffn_W2, L0_ffn_W3, L1_xattn_Wq, L1_xattn_bq, L1_xattn_Wk, L1_xattn_bk, L1_xattn_Wv, L1_xattn_bv, L1_xattn_beta_risk, L1_xattn_beta_prio, L1_xattn_beta_impl, L1_ffn_weight, L1_ffn_aux_weight1, L1_ffn_aux_weight2, L1_ffn_bias):
    import jax
    import jax.numpy as jnp

    def _L0_xattn_ref(x, context, mask, Wq, Wkv, Wout, b_out):
        import jax, jax.numpy as jnp
        import numpy as np
        HEADS = 16
        DIM_HEAD = 64
        SCALE = DIM_HEAD ** (-0.5)
        B, Nq, _ = x.shape
        Nkv = context.shape[1]
        q = x @ Wq.T
        kv = context @ Wkv.T
        k, v = jnp.split(kv, 2, axis=-1)
        q = q.reshape(B, Nq, HEADS, DIM_HEAD).transpose(0, 2, 1, 3)
        k = k.reshape(B, Nkv, HEADS, DIM_HEAD).transpose(0, 2, 1, 3)
        v = v.reshape(B, Nkv, HEADS, DIM_HEAD).transpose(0, 2, 1, 3)
        sim = jnp.einsum('bhid,bhjd->bhij', q, k) * SCALE
        max_neg = -jnp.finfo(sim.dtype).max
        sim = jnp.where(mask[:, None, None, :], sim, max_neg)
        attn = jax.nn.softmax(sim, axis=-1)
        out = jnp.einsum('bhij,bhjd->bhid', attn, v)
        out = out.transpose(0, 2, 1, 3).reshape(B, Nq, HEADS * DIM_HEAD)
        return out @ Wout.T + b_out

    def _L0_ffn_ref(x, Wg, W1, W2, W3):
        import jax, jax.numpy as jnp
        import numpy as np
        B, T, C, H, E = (4, 512, 256, 512, 8)
        CAPACITY_FACTOR = 1.0
        b, t, c = x.shape
        e = Wg.shape[0]
        n = b * t
        capacity = max(1, int(CAPACITY_FACTOR * n / e))
        x_flat = x.reshape(n, c)
        scores = (x_flat @ Wg.T).T
        top_vals, token_idx = jax.lax.top_k(scores, capacity)
        token_w = jax.nn.softmax(top_vals, axis=-1)
        xg = x_flat[token_idx]
        h = jax.nn.silu(jnp.einsum('eic,ehc->eih', xg, W1)) * jnp.einsum('eic,ehc->eih', xg, W3)
        y = jnp.einsum('eih,ech->eic', h, W2) * token_w[..., None]
        out = jnp.zeros_like(x_flat).at[token_idx.reshape(-1)].add(y.reshape(-1, c))
        return out.reshape(b, t, c)

    def _L1_xattn_ref(q_in, k_in, v_in, phi_risk, phi_prio, phi_impl, Wq, bq, Wk, bk, Wv, bv, beta_risk, beta_prio, beta_impl):
        import jax, jax.numpy as jnp
        import numpy as np
        D = 256
        d = q_in.shape[-1]
        scale = jnp.asarray(d, q_in.dtype) ** (-0.5)
        Q = q_in @ Wq.T + bq
        K = k_in @ Wk.T + bk
        V = v_in @ Wv.T + bv
        att = jnp.einsum('bsd,btd->bst', Q, K) * scale
        att = att + beta_risk * phi_risk + beta_prio * phi_prio - beta_impl * phi_impl
        w = jax.nn.softmax(att, axis=-1)
        return jnp.einsum('bst,btd->bsd', w, V)

    def _L1_ffn_ref(x, weight, aux_weight1, aux_weight2, bias):
        import jax, jax.numpy as jnp
        import numpy as np
        D_MODEL = 256
        h = jnp.einsum('btc,cd->btd', x, weight)
        h = jnp.einsum('btc,cd->btd', h, aux_weight1)
        h = jnp.einsum('btc,cd->btd', h, aux_weight2)
        return jnp.tanh(h + bias)
    x = x + _L0_xattn_ref(_layernorm(x, axis=-1), ctx_1024, mask_BxS2_bf1, L0_xattn_Wq, L0_xattn_Wkv, L0_xattn_Wout, L0_xattn_b_out)
    x = x + _L0_ffn_ref(_layernorm(x, axis=-1), L0_ffn_Wg, L0_ffn_W1, L0_ffn_W2, L0_ffn_W3)
    x = x + _L1_xattn_ref(_layernorm(x, axis=-1), ctx_1024, ctx_1024, fside_BxSxS2_0, fside_BxSxS2_0, fside_BxSxS2_0, L1_xattn_Wq, L1_xattn_bq, L1_xattn_Wk, L1_xattn_bk, L1_xattn_Wv, L1_xattn_bv, L1_xattn_beta_risk, L1_xattn_beta_prio, L1_xattn_beta_impl)
    x = x + _L1_ffn_ref(_layernorm(x, axis=-1), L1_ffn_weight, L1_ffn_aux_weight1, L1_ffn_aux_weight2, L1_ffn_bias)
    return x

_drawn_inputs = setup_inputs


def setup_inputs(seed=0):
    import zlib

    import numpy as np

    out = dict(_drawn_inputs(seed))
    spreads = {'L0_xattn_b_out': (0.0, 0.1), 'L1_ffn_bias': (0.0, 0.1)}
    factors = {'fside_BxSxS2_0': 5.965,
     'L0_ffn_Wg': 8.0,
     'L0_ffn_W1': 8.0,
     'L0_ffn_W2': 8.0,
     'L0_ffn_W3': 8.0,
     'L1_xattn_bq': 36.11,
     'L1_xattn_bk': 64.0,
     'L1_xattn_bv': 7.238}
    for name, (base, spread) in spreads.items():
        noise = np.random.default_rng([zlib.crc32(name.encode()), seed]).standard_normal(out[name].shape)
        drawn = base * np.exp(spread * noise) if base else spread * noise
        out[name] = jnp.asarray(drawn.astype(out[name].dtype))
    for name, factor in factors.items():
        out[name] = (out[name] * factor).astype(out[name].dtype)
    return out
```

```python
from contextlib import ExitStack

import concourse.bass as bass
from concourse import mybir

ALU = mybir.AluOpType
ACT = mybir.ActivationFunctionType
AX = mybir.AxisListType
F32 = mybir.dt.float32
F32R = mybir.dt.float32r
I32 = mybir.dt.int32
U32 = mybir.dt.uint32
U8 = mybir.dt.uint8
BF16 = mybir.dt.bfloat16

P = 128
B, S, D = 16, 256, 256
J = 120
H, DH = 16, 64
INNER = H * DH
TT = S // P
KD = D // P
MI = INNER // P
GROUPS = 4
HG = H // GROUPS
NT = B * TT
E, CAP, HID = 8, 512, 512
EPS = 1e-5
NEG = -3.0e38


class Batch:

    def __init__(self, i, c):
        self.i, self.c, self.par = i, c, c % 2
        self.turn = i + c // 2
        self.n = 2 * i + c

    def shift(self, d):
        return Batch(self.i, self.c + d)

    def real(self):
        return not isinstance(self.n, int) or 0 <= self.n < B

    def at_least(self, n):
        return not isinstance(self.n, int) or self.n >= n


class Batch4:

    def __init__(self, i, c):
        self.i, self.c, self.n = i, c, 4 * i + c

    def turn(self, ring):
        return (4 // ring) * self.i + self.c // ring

    def shift(self, d):
        return Batch4(self.i, self.c + d)

    def real(self):
        return not isinstance(self.n, int) or 0 <= self.n < B

    def at_least(self, n):
        return not isinstance(self.n, int) or self.n >= n


def pipeline(eng, body):
    for n in range(-1, 4):
        body(Batch(0, n))
    with eng.Fori(2, (B - 2) // 2) as i:
        for c in range(2):
            body(Batch(i, c))
    for n in range(B - 2, B + 2):
        body(Batch(0, n))


def first_attention(nc, io, x1_dram, xn1_dram, ident, scores):
    with ExitStack() as ctx:
        def sb(name, shape, dt=F32):
            return ctx.enter_context(nc.sbuf_tensor("a_" + name, shape, dt))

        def ps(name):
            return ctx.enter_context(nc.psum_tensor("ap_" + name, [P, 512], F32))

        def sem(name):
            return ctx.enter_context(nc.semaphore("a_" + name))

        wq = [sb(f"wq{s}", [P, KD, INNER], F32R) for s in ("hi", "lo")]
        wv = [sb(f"wv{s}", [P, KD, INNER], F32R) for s in ("hi", "lo")]
        wo = [sb(f"wo{s}", [P, MI, D], F32R) for s in ("hi", "lo")]
        wk = sb("wk", [P, KD, INNER])
        stage = [sb(f"stage{n}", [P, KD * INNER]) for n in range(2)]
        wgt = sb("wgt", [P, KD, E])
        bout = sb("bout", [P, D])
        neghalf = sb("neghalf", [P, TT])
        turnstile = sb("turnstile", [P, 1])
        xin = [sb(f"xin{n}", [P, TT, D]) for n in range(2)]
        xres = [sb(f"xres{n}", [P, TT, D]) for n in range(2)]
        ctxt = [sb(f"ctxt{n}", [P, KD, J]) for n in range(2)]
        ctxh = [sb(f"ctxh{n}", [P, KD, J], F32R) for n in range(2)]
        ctxl = [sb(f"ctxl{n}", [P, KD, J], F32R) for n in range(2)]
        mask8 = sb("mask8", [P, B * J], U8)
        bias = sb("bias", [P, B, J], BF16)
        xn = sb("xn", [P, TT, D])
        xnh = sb("xnh", [P, KD, S], F32R)
        xnl = sb("xnl", [P, KD, S], F32R)
        qt = [sb(f"qt{n}", [P, MI, S]) for n in range(2)]
        kt = [sb(f"kt{n}", [P, MI, J]) for n in range(2)]
        vh = [sb(f"vh{n}", [J, INNER], F32R) for n in range(2)]
        vl = [sb(f"vl{n}", [J, INNER], F32R) for n in range(2)]
        prob = [sb(f"prob{n}", [P, 2, TT * 2, J]) for n in range(4)]
        negmax = [sb(f"negmax{n}", [P, 2, TT * 2]) for n in range(2)]
        den = [sb(f"den{n}", [P, 2, TT * 2]) for n in range(2)]
        rden = [sb(f"rden{n}", [P, 2, TT * 2]) for n in range(2)]
        pth = [sb(f"pth{n}", [J, 2, 2, S], F32R) for n in range(2)]
        ptl = [sb(f"ptl{n}", [J, 2, 2, S], F32R) for n in range(2)]
        oth = sb("oth", [P, MI, S], F32R)
        otl = sb("otl", [P, MI, S], F32R)
        x1 = [sb(f"x1{n}", [P, TT, D]) for n in range(2)]
        xn1 = [sb(f"xn1{n}", [P, TT, D]) for n in range(2)]
        x1t = sb("x1t", [P, KD, S])
        bn = [sb(f"bn{n}", [P, TT, 6]) for n in range(2)]
        mv = [sb(f"mv{n}", [P, TT, 2]) for n in range(2)]
        var = [sb(f"var{n}", [P, TT]) for n in range(2)]
        rstd = [sb(f"rstd{n}", [P, TT]) for n in range(2)]

        sim_ps = [ps("sim0"), ps("sim1")]
        t_ps = [ps("t0"), ps("t1")]
        pv_ps = [ps("pv0"), ps("pv1")]
        job_ps = [ps("job0"), ps("job1")]

        w_in = [sem(f"w_in{n}") for n in range(2)]
        wk_in, small_in = sem("wk_in"), sem("small_in")
        w_hi, w_lo = sem("w_hi"), sem("w_lo")
        x_in = [sem(f"x_in{n}") for n in range(2)]
        xres_in = [sem(f"xres_in{n}") for n in range(2)]
        ctx_in = [sem(f"ctx_in{n}") for n in range(2)]
        mask_in = sem("mask_in")
        half_set = sem("half_set")
        ctx_hi, ctx_lo, bias_set = sem("ctx_hi"), sem("ctx_lo"), sem("bias_set")
        bn_done = [sem("bn_x"), sem("bn_x1")]
        mv_done = [sem("mv_x"), sem("mv_x1")]
        var_done = [sem("var_x"), sem("var_x1")]
        rstd_done = [sem("rstd_x"), sem("rstd_x1")]
        xn_done, x1_done, xn1_done, yb_done = sem("xn_done"), sem("x1_done"), sem("xn1_done"), sem("yb_done")
        kinds = ("xt", "v", "k", "q", "y", "x1t", "gate")
        made = {k: sem("made_" + k) for k in kinds}
        out = {k: sem("out_" + k) for k in kinds}
        xt_hi, v_hi = sem("xt_hi"), sem("v_hi")
        sim_done, biased, maxed, shifted = sem("sim_done"), sem("biased"), sem("maxed"), sem("shifted")
        exped, summed, inverted, normed = sem("exped"), sem("summed"), sem("inverted"), sem("normed")
        pt_made, pt_hi, pt_lo = sem("pt_made"), sem("pt_hi"), sem("pt_lo")
        pv_done, o_hi, o_lo = sem("pv_done"), sem("o_hi"), sem("o_lo")
        x1_stored = [sem(f"x1_stored{n}") for n in range(2)]
        xn1_stored = [sem(f"xn1_stored{n}") for n in range(2)]

        x_dram = io["x"].rearrange("b (t p) c -> b p t c", p=P)
        x1_out = x1_dram.rearrange("(b t p) c -> b p t c", p=P, t=TT)
        xn1_out = xn1_dram.rearrange("(b t p) c -> b p t c", p=P, t=TT)

        JOBS = [[("xt", 1, 0), ("k", 1, 0), ("k", 1, 1)],
                [("q", 1, 0), ("q", 1, 1), ("x1t", -2, 0)],
                [("q", 1, 2), ("y", -1, 0), ("v", 1, 0)],
                [("q", 1, 3), ("v", 1, 1), ("gate", -2, 0)]]
        PARTS = {"xt": 1, "v": 2, "k": 2, "q": 4, "y": 1, "x1t": 1, "gate": 1}
        flat = [job for step in JOBS for job in step]

        def job_bank(g, n):
            return job_ps[(3 * g + n) % 2]

        def before_last(beta, g, n):
            for at in range(3 * g + n - 2, -2 * len(flat), -2):
                kind, rel, part = flat[at % len(flat)]
                b = beta.shift(rel + at // len(flat))
                if b.real():
                    return kind, b, part
            return None

        def count(kind, b, part):
            return PARTS[kind] * b.n + part + 1

        def groups(beta, g):
            late = (beta.shift(-1), g + 2) if g < 2 else (beta, g - 2)
            return (beta, g), late

        def nth(b, g):
            return GROUPS * b.n + g

        block = ctx.enter_context(nc.Block())

        @block.sync
        def _(sp):
            sp.dma_start(bout[:, :], io["bout"].rearrange("(a c) -> a c", a=1).to_broadcast([P, D])).then_inc(small_in, 16)
            sp.dma_start(wgt[:, :, :], io["wgt"]).then_inc(small_in, 16)
            sp.dma_start(mask8[:, :], io["mask"].rearrange("(a b) j -> a (b j)", a=1).to_broadcast([P, B * J])).then_inc(mask_in, 16)
            sp.dma_start(wk[:, :, :], io["wkt"]).then_inc(wk_in, 16)

            def loads(b):
                p = b.par
                if b.at_least(2):
                    sp.wait_ge(xn_done, b.n - 1)
                sp.dma_start(xin[p][:, :, :], x_dram[b.n]).then_inc(x_in[p], 16)
                if b.at_least(2):
                    sp.wait_ge(made["k"], 2 * (b.n - 1))
                    sp.wait_ge(ctx_lo, b.n - 1)
                sp.dma_start(ctxt[p][:, :, :], io["ctxt"][b.n]).then_inc(ctx_in[p], 16)

            def load_residual(b):
                if b.at_least(2):
                    sp.wait_ge(x1_done, b.n - 1)
                sp.dma_start(xres[b.par][:, :, :], x_dram[b.n]).then_inc(xres_in[b.par], 16)

            loads(Batch(0, 0))
            sp.dma_start(stage[0][:, :], io["wqt"]).then_inc(w_in[0], 16)
            sp.dma_start(stage[1][:, :], io["wvt"]).then_inc(w_in[1], 16)
            loads(Batch(0, 1))
            sp.wait_ge(w_lo, 1)
            sp.dma_start(stage[0][:, :], io["wot"]).then_inc(w_in[0], 16)

            def block_of(beta):
                if beta.shift(2).real() and beta.shift(2).at_least(2):
                    loads(beta.shift(2))
                b = beta.shift(-2)
                if b.real():
                    sp.wait_ge(x1_done, b.n + 1)
                    sp.dma_start(x1_out[b.n], x1[b.par][:, :, :]).then_inc(x1_stored[b.par], 16)
                    sp.wait_ge(xn1_done, b.n + 1)
                    sp.dma_start(xn1_out[b.n], xn1[b.par][:, :, :]).then_inc(xn1_stored[b.par], 16)
                if beta.shift(1).real():
                    load_residual(beta.shift(1))

            pipeline(sp, block_of)
            for n in range(2):
                sp.wait_ge(x1_stored[n], 16 * (B // 2))
                sp.wait_ge(xn1_stored[n], 16 * (B // 2))

        @block.tensor
        def _(pe):
            def mm3(out_ap, lhs, rhs, start, stop):
                (lh, ll), (rh, rl) = lhs, rhs
                nc.tensor.matmul(out_ap, lh, rh, start=start, stop=False)
                nc.tensor.matmul(out_ap, lh, rl, start=False, stop=False)
                return nc.tensor.matmul(out_ap, ll, rh, start=False, stop=stop)

            def job(beta, g, n):
                kind, rel, part = JOBS[g][n]
                b = beta.shift(rel)
                if not b.real():
                    return
                before = before_last(beta, g, n)
                if before:
                    pe.wait_ge(out[before[0]], count(*before))
                bank, p = job_bank(g, n), b.par
                if kind == "xt":
                    pe.wait_ge(xn_done, b.n + 1)
                    for t in range(TT):
                        for k in range(KD):
                            last = nc.tensor.transpose(bank[:, k * S + t * P:k * S + (t + 1) * P],
                                                       xn[:, t, k * P:(k + 1) * P], ident[:, :])
                elif kind == "v":
                    if part == 0:
                        pe.wait_ge(ctx_hi, b.n + 1)
                        pe.wait_ge(ctx_lo, b.n + 1)
                        if not b.at_least(1):
                            pe.wait_ge(w_hi, 2)
                            pe.wait_ge(w_lo, 2)
                    for k in range(KD):
                        cols = slice(part * 512, part * 512 + 512)
                        last = mm3(bank[0:J, :], (ctxh[p][:, k, :], ctxl[p][:, k, :]),
                                   (wv[0][:, k, cols], wv[1][:, k, cols]), k == 0, k == KD - 1)
                elif kind == "k":
                    if part == 0:
                        pe.wait_ge(ctx_in[p], 16 * (b.turn + 1))
                        if not b.at_least(1):
                            pe.wait_ge(wk_in, 16)
                    for m in range(4):
                        for k in range(KD):
                            mi = 4 * part + m
                            last = nc.tensor.matmul(bank[:, m * J:(m + 1) * J], wk[:, k, mi * P:(mi + 1) * P],
                                                    ctxt[p][:, k, :], start=k == 0, stop=k == KD - 1)
                elif kind == "q":
                    if part == 0:
                        pe.wait_ge(xt_hi, b.n + 1)
                        pe.wait_ge(out["xt"], b.n + 1)
                        if not b.at_least(1):
                            pe.wait_ge(w_hi, 1)
                            pe.wait_ge(w_lo, 1)
                    for m in range(2):
                        mi = 2 * part + m
                        cols = slice(mi * P, mi * P + P)
                        for k in range(KD):
                            last = mm3(bank[:, m * S:(m + 1) * S], (wq[0][:, k, cols], wq[1][:, k, cols]),
                                       (xnh[:, k, :], xnl[:, k, :]), k == 0, k == KD - 1)
                elif kind == "y":
                    pe.wait_ge(o_hi, 2 * nth(b, GROUPS))
                    pe.wait_ge(o_lo, 2 * nth(b, GROUPS))
                    if not b.at_least(1):
                        pe.wait_ge(w_hi, 3)
                        pe.wait_ge(w_lo, 3)
                    for t in range(TT):
                        rows = slice(t * P, (t + 1) * P)
                        for m in range(MI):
                            last = mm3(bank[:, t * D:(t + 1) * D], (oth[:, m, rows], otl[:, m, rows]),
                                       (wo[0][:, m, :], wo[1][:, m, :]), m == 0, m == MI - 1)
                elif kind == "x1t":
                    pe.wait_ge(xn1_done, b.n + 1)
                    for t in range(TT):
                        for k in range(KD):
                            last = nc.tensor.transpose(bank[:, k * S + t * P:k * S + (t + 1) * P],
                                                       xn1[p][:, t, k * P:(k + 1) * P], ident[:, :])
                else:
                    pe.wait_ge(out["x1t"], b.n + 1)
                    for t in range(TT):
                        for k in range(KD):
                            last = nc.tensor.matmul(bank[:, t * E:(t + 1) * E], x1t[:, k, t * P:(t + 1) * P],
                                                    wgt[:, k, :], start=k == 0, stop=k == KD - 1)
                last.then_inc(made[kind], 1)

            def sim(b, g):
                pe.wait_ge(out["k"], 2 * b.n + g // 2 + 1)
                pe.wait_ge(out["q"], 4 * b.n + g + 1)
                n = nth(b, g)
                if g or b.at_least(1):
                    pe.wait_ge(biased, 2 * n)
                for t in range(TT):
                    for hh in range(2):
                        for odd in range(2):
                            m, rows = 2 * g + hh, slice(DH * odd, DH * odd + DH)
                            at = (t * 2 + hh) * J
                            last = nc.tensor.matmul(sim_ps[odd][:, at:at + J], qt[b.par][rows, m, t * P:(t + 1) * P],
                                                    kt[b.par][rows, m, :], start=True, stop=True)
                            if t == TT - 1 and hh == 1:
                                last.then_inc(sim_done, 1)

            def transposes(b, g):
                n = nth(b, g)
                for odd in range(2):
                    pe.wait_ge(normed, 2 * n + odd + 1)
                    if g or b.at_least(1):
                        pe.wait_ge(pt_lo, 2 * n - 2 + odd + 1)
                    for hh in range(2):
                        for t in range(TT):
                            last = nc.tensor.transpose(t_ps[odd][0:J, hh * S + t * P:hh * S + (t + 1) * P],
                                                       prob[g % 4][:, odd, t * 2 + hh, :], ident[:, :])
                    last.then_inc(pt_made, 1)

            def values(b, g):
                n = nth(b, g)
                if g == 0:
                    pe.wait_ge(v_hi, 2 * b.n + 2)
                    pe.wait_ge(out["v"], 2 * b.n + 2)
                for odd in range(2):
                    pe.wait_ge(pt_hi, 2 * n + odd + 1)
                    pe.wait_ge(pt_lo, 2 * n + odd + 1)
                    if g or b.at_least(1):
                        pe.wait_ge(o_lo, 2 * n - 2 + odd + 1)
                    for hh in range(2):
                        h = HG * g + 2 * hh + odd
                        cols = slice(h * DH, h * DH + DH)
                        last = mm3(pv_ps[odd][0:DH, hh * S:(hh + 1) * S], (vh[b.par][:, cols], vl[b.par][:, cols]),
                                   (pth[g % 2][:, odd, hh, :], ptl[g % 2][:, odd, hh, :]), True, True)
                    last.then_inc(pv_done, 1)

            def block_of(beta):
                for g in range(GROUPS):
                    (b, g1), (b2, g2) = groups(beta, g)
                    if b.real():
                        sim(b, g1)
                    if b2.real():
                        transposes(b2, g2)
                    for n in range(3):
                        job(beta, g, n)
                    if b2.real():
                        values(b2, g2)

            pipeline(pe, block_of)

        @block.scalar
        def _(act):
            for n, (w, s) in enumerate(((wq, 0), (wv, 1), (wo, 0))):
                act.wait_ge(w_in[s], 16 * (n // 2 + 1))
                nc.scalar.copy(w[0][:, :, :].rearrange("p a b -> p (a b)"), stage[s][:, :]).then_inc(w_hi, 1)
                if n == 0:
                    act.wait_ge(ctx_in[0], 16)
                    nc.scalar.copy(ctxh[0][:, :, :], ctxt[0][:, :, :]).then_inc(ctx_hi, 1)
                    act.wait_ge(ctx_in[1], 16)
                    nc.scalar.copy(ctxh[1][:, :, :], ctxt[1][:, :, :]).then_inc(ctx_hi, 1)

            def job(beta, g, n):
                kind, rel, part = JOBS[g][n]
                b = beta.shift(rel)
                if not b.real() or kind in ("y", "gate"):
                    return
                bank, p = job_bank(g, n), b.par
                act.wait_ge(made[kind], count(kind, b, part))
                if kind == "xt":
                    if b.at_least(1):
                        act.wait_ge(made["q"], 4 * b.n)
                    nc.scalar.copy(xnh[:, :, :].rearrange("p a b -> p (a b)"), bank[:, :]).then_inc(xt_hi, 1)
                elif kind == "v":
                    if part == 0 and b.at_least(2):
                        act.wait_ge(pv_done, 2 * nth(b.shift(-2), GROUPS))
                    nc.scalar.copy(vh[p][:, part * 512:part * 512 + 512], bank[0:J, :]).then_inc(v_hi, 1)
                elif kind == "k":
                    if part == 0 and b.at_least(2):
                        act.wait_ge(sim_done, 2 * nth(b.shift(-2), GROUPS))
                    nc.scalar.copy(kt[p][:, 4 * part:4 * part + 4, :].rearrange("p a b -> p (a b)"),
                                   bank[:, 0:4 * J]).then_inc(out["k"], 1)
                elif kind == "q":
                    if part == 0 and b.at_least(2):
                        act.wait_ge(sim_done, 2 * nth(b.shift(-2), GROUPS))
                    nc.scalar.copy(qt[p][:, 2 * part:2 * part + 2, :].rearrange("p a b -> p (a b)"),
                                   bank[:, :]).then_inc(out["q"], 1)
                elif kind == "x1t":
                    if b.at_least(1):
                        act.wait_ge(made["gate"], b.n)
                    nc.scalar.copy(x1t[:, :, :].rearrange("p a b -> p (a b)"), bank[:, :]).then_inc(out["x1t"], 1)

            def pt_leading(b, g):
                n = nth(b, g)
                for odd in range(2):
                    act.wait_ge(pt_made, 2 * n + odd + 1)
                    if b.at_least(1) or g >= 2:
                        act.wait_ge(pv_done, 2 * (n - 2) + odd + 1)
                    nc.scalar.copy(pth[g % 2][:, odd, :, :].rearrange("p a b -> p (a b)"),
                                   t_ps[odd][0:J, :]).then_inc(pt_hi, 1)

            def out_leading(b, g):
                n = nth(b, g)
                if g == 0 and b.at_least(1):
                    act.wait_ge(made["y"], b.n)
                for odd in range(2):
                    act.wait_ge(pv_done, 2 * n + odd + 1)
                    nc.scalar.copy(oth[DH * odd:DH * odd + DH, 2 * g:2 * g + 2, :].rearrange("p a b -> p (a b)"),
                                   pv_ps[odd][0:DH, :]).then_inc(o_hi, 1)

            def exps(b, g):
                n = nth(b, g)
                for odd in range(2):
                    act.wait_ge(shifted, 2 * n + odd + 1)
                    ap = prob[g % 4][:, odd, :, :]
                    nc.scalar.activation(ap, ap, ACT.Exp, scale=DH ** -0.5).then_inc(exped, 1)

            def block_of(beta):
                for g in range(GROUPS):
                    (b, g1), (b2, g2) = groups(beta, g)
                    if b2.real():
                        pt_leading(b2, g2)
                    for n in range(2):
                        job(beta, g, n)
                    if b.real():
                        exps(b, g1)
                    job(beta, g, 2)
                    if b2.real():
                        out_leading(b2, g2)
                    if g == 1 and beta.shift(2).real() and beta.shift(2).at_least(2):
                        c = beta.shift(2)
                        act.wait_ge(ctx_in[c.par], 16 * (c.turn + 1))
                        act.wait_ge(made["v"], 2 * (c.n - 1))
                        nc.scalar.copy(ctxh[c.par][:, :, :], ctxt[c.par][:, :, :]).then_inc(ctx_hi, 1)

            pipeline(act, block_of)

        @block.gpsimd
        def _(pool):
            pool.memset(neghalf[:, :], -0.5).then_inc(half_set, 1)
            pool.wait_ge(half_set, 1)

            def rsqrt(which, b):
                pool.wait_ge(var_done[which], b.n + 1)
                nc.gpsimd.tensor_tensor(rstd[which][:, :], var[which][:, :], neghalf[:, :],
                                        ALU.pow).then_inc(rstd_done[which], 1)

            def shift(b, g):
                n = nth(b, g)
                for odd in range(2):
                    pool.wait_ge(maxed, 2 * n + odd + 1)
                    ap = prob[g % 4][:, odd, :, :]
                    nc.gpsimd.tensor_tensor(ap, ap, negmax[g % 2][:, odd, :].unsqueeze(2).to_broadcast([P, TT * 2, J]),
                                            ALU.add).then_inc(shifted, 1)

            def normalise(b, g):
                n = nth(b, g)
                pool.wait_ge(inverted, n + 1)
                for odd in range(2):
                    ap = prob[g % 4][:, odd, :, :]
                    nc.gpsimd.tensor_tensor(ap, ap, rden[g % 2][:, odd, :].unsqueeze(2).to_broadcast([P, TT * 2, J]),
                                            ALU.mult).then_inc(normed, 1)

            rsqrt(0, Batch(0, 0))

            def block_of(beta):
                for g in range(GROUPS):
                    (b, g1), _ = groups(beta, g)
                    if b.real():
                        shift(b, g1)
                    if g == 0 and beta.shift(-1).real():
                        normalise(beta.shift(-1), GROUPS - 1)
                    if g and b.real():
                        normalise(b, g - 1)
                    if g == 2 and beta.shift(2).real() and beta.shift(2).at_least(1):
                        rsqrt(0, beta.shift(2))
                    if g == 2 and beta.shift(-1).real():
                        rsqrt(1, beta.shift(-1))

            pipeline(pool, block_of)

        @block.vector
        def _(dve):
            def lower(out_ap, whole, hi, signal):
                return nc.vector.tensor_tensor(out_ap, whole, hi.bitcast(F32), ALU.subtract).then_inc(signal, 1)

            def statistics(which, b, src):
                for t in range(TT):
                    last = nc.vector.bn_stats(bn[which][:, t, :], src[:, t, :])
                last.then_inc(bn_done[which], 1)
                dve.wait_ge(bn_done[which], b.n + 1)
                nc.vector.memset(turnstile[:, :], 0.0)
                for t in range(TT):
                    last = nc.vector.bn_aggr(mv[which][:, t, :], bn[which][:, t, :])
                last.then_inc(mv_done[which], 1)
                dve.wait_ge(mv_done[which], b.n + 1)
                nc.vector.tensor_scalar(var[which][:, :], mv[which][:, :, 1], EPS, None, ALU.add).then_inc(var_done[which], 1)

            def normal(which, b, src, dst, signal):
                dve.wait_ge(rstd_done[which], b.n + 1)
                for t in range(TT):
                    last = nc.vector.tensor_scalar(dst[:, t, :], src[:, t, :], mv[which][:, t, 0:1], rstd[which][:, t:t + 1],
                                                   ALU.subtract, ALU.mult)
                last.then_inc(signal, 1)

            def normal_x(b):
                if b.at_least(1):
                    dve.wait_ge(made["xt"], b.n)
                normal(0, b, xin[b.par], xn, xn_done)

            def split_context(b):
                dve.wait_ge(ctx_hi, b.n + 1)
                lower(ctxl[b.par][:, :, :], ctxt[b.par][:, :, :], ctxh[b.par][:, :, :], ctx_lo)

            dve.wait_ge(mask_in, 16)
            nc.vector.tensor_scalar(bias[:, :, :].rearrange("p b j -> p (b j)"), mask8[:, :], -NEG, NEG, ALU.mult, ALU.add).then_inc(bias_set, 1)
            dve.wait_ge(x_in[0], 16)
            statistics(0, Batch(0, 0), xin[0])
            for n, (w, s) in enumerate(((wq, 0), (wv, 1), (wo, 0))):
                dve.wait_ge(w_hi, n + 1)
                lower(w[1][:, :, :].rearrange("p a b -> p (a b)"), stage[s][:, :],
                      w[0][:, :, :].rearrange("p a b -> p (a b)"), w_lo)
                if n == 0:
                    normal_x(Batch(0, 0))
                    split_context(Batch(0, 0))
                    split_context(Batch(0, 1))
            dve.wait_ge(small_in, 32)

            def job(beta, g, n):
                kind, rel, part = JOBS[g][n]
                b = beta.shift(rel)
                if not b.real() or kind not in ("xt", "v", "y", "gate"):
                    return
                bank, p = job_bank(g, n), b.par
                if kind == "xt":
                    dve.wait_ge(xt_hi, b.n + 1)
                    lower(xnl[:, :, :].rearrange("p a b -> p (a b)"), bank[:, :],
                          xnh[:, :, :].rearrange("p a b -> p (a b)"), out["xt"])
                elif kind == "v":
                    dve.wait_ge(v_hi, 2 * b.n + part + 1)
                    cols = slice(part * 512, part * 512 + 512)
                    lower(vl[p][:, cols], bank[0:J, :], vh[p][:, cols], out["v"])
                elif kind == "y":
                    dve.wait_ge(made["y"], b.n + 1)
                    dve.wait_ge(xres_in[p], 16 * (b.turn + 1))
                    if b.at_least(2):
                        dve.wait_ge(x1_stored[p], 16 * b.turn)
                    nc.vector.tensor_tensor(x1[p][:, :, :], bank[:, :].rearrange("p (t c) -> p t c", t=TT),
                                            xres[p][:, :, :], ALU.add).then_inc(out["y"], 1)
                    dve.wait_ge(out["y"], b.n + 1)
                    nc.vector.tensor_tensor(x1[p][:, :, :], x1[p][:, :, :],
                                            bout[:, :].unsqueeze(1).to_broadcast([P, TT, D]), ALU.add).then_inc(x1_done, 1)
                    dve.wait_ge(x1_done, b.n + 1)
                    statistics(1, b, x1[p])
                else:
                    dve.wait_ge(made["gate"], b.n + 1)
                    nc.vector.tensor_copy(scores[:, :, bass.ds(TT * b.n, TT)].rearrange("p e t -> p t e"),
                                          bank[:, 0:TT * E].rearrange("p (t e) -> p t e", t=TT)).then_inc(out["gate"], 1)

            def add_bias(b, g):
                n = nth(b, g)
                if g == 0 and not b.at_least(1):
                    dve.wait_ge(bias_set, 1)
                for odd in range(2):
                    dve.wait_ge(sim_done, 2 * n + odd + 1)
                    if b.at_least(1):
                        dve.wait_ge(pt_made, 2 * (n - 4) + odd + 1)
                    nc.vector.tensor_tensor(prob[g % 4][:, odd, :, :], sim_ps[odd][:, 0:4 * J].rearrange("p (a j) -> p a j", j=J),
                                            bias[:, bass.ds(b.n, 1), :].to_broadcast([P, 4, J]), ALU.add).then_inc(biased, 1)

            def maxima(b, g):
                n = nth(b, g)
                for odd in range(2):
                    dve.wait_ge(biased, 2 * n + odd + 1)
                    if b.at_least(1) or g >= 2:
                        dve.wait_ge(shifted, 2 * (n - 2) + odd + 1)
                    nc.vector.tensor_reduce(negmax[g % 2][:, odd, :], prob[g % 4][:, odd, :, :], AX.X, ALU.max,
                                            negate=True).then_inc(maxed, 1)

            def sums(b, g):
                n = nth(b, g)
                dve.wait_ge(exped, 2 * n + 2)
                if b.at_least(1) or g >= 1:
                    dve.wait_ge(normed, 2 * n)
                nc.vector.tensor_reduce(den[g % 2][:, :, :], prob[g % 4][:, :, :, :], AX.X, ALU.add).then_inc(summed, 1)
                dve.wait_ge(summed, n + 1)
                nc.vector.reciprocal(rden[g % 2][:, :, :], den[g % 2][:, :, :]).then_inc(inverted, 1)

            def pt_rest(b, g):
                n = nth(b, g)
                for odd in range(2):
                    dve.wait_ge(pt_hi, 2 * n + odd + 1)
                    lower(ptl[g % 2][:, odd, :, :].rearrange("p a b -> p (a b)"), t_ps[odd][0:J, :],
                          pth[g % 2][:, odd, :, :].rearrange("p a b -> p (a b)"), pt_lo)

            def out_rest(b, g):
                n = nth(b, g)
                for odd in range(2):
                    dve.wait_ge(o_hi, 2 * n + odd + 1)
                    rows = slice(DH * odd, DH * odd + DH)
                    lower(otl[rows, 2 * g:2 * g + 2, :].rearrange("p a b -> p (a b)"), pv_ps[odd][0:DH, :],
                          oth[rows, 2 * g:2 * g + 2, :].rearrange("p a b -> p (a b)"), o_lo)

            def block_of(beta):
                for g in range(GROUPS):
                    (b, g1), (b2, g2) = groups(beta, g)
                    if b.real():
                        add_bias(b, g1)
                    if g == 0:
                        job(beta, g, 0)
                    if b2.real():
                        pt_rest(b2, g2)
                    if b.real():
                        maxima(b, g1)
                    before = (b.shift(-1), GROUPS - 1) if g == 0 else (b, g - 1)
                    if before[0].real():
                        sums(*before)
                    if g == 3 and beta.shift(2).real() and beta.shift(2).at_least(1):
                        normal_x(beta.shift(2))
                    for n in range(g == 0, 2):
                        job(beta, g, n)
                    job(beta, g, 2)
                    if b2.real():
                        out_rest(b2, g2)
                    c, d = beta.shift(2), beta.shift(-1)
                    if g == 1 and c.real() and c.at_least(1):
                        dve.wait_ge(x_in[c.par], 16 * (c.turn + 1))
                        statistics(0, c, xin[c.par])
                        if c.at_least(2):
                            split_context(c)
                    if g == 3 and d.real():
                        if d.at_least(2):
                            dve.wait_ge(xn1_stored[d.par], 16 * d.turn)
                            dve.wait_ge(made["x1t"], d.n - 1)
                        normal(1, d, x1[d.par], xn1[d.par], xn1_done)

            pipeline(dve, block_of)


def route(nc, io, scores, slots_dram, expert_max, expert_inv, second):
    gt, keys_m, keys_bias, values, ffn_w = second
    with ExitStack() as ctx:
        def sb(name, shape, dt=F32):
            return ctx.enter_context(nc.sbuf_tensor("r_" + name, shape, dt))

        def ps(name):
            return ctx.enter_context(nc.psum_tensor("rp_" + name, [P, 512], F32))

        def sem(name):
            return ctx.enter_context(nc.semaphore("r_" + name))

        wide = [P, E, NT]
        ones = sb("ones", [P, P], BF16)
        tri = sb("tri", [P, P], BF16)
        keep = sb("keep", [P, E, NT])
        iota = sb("iota", [P, 32], I32)
        row = sb("row", [P, 1], I32)
        tile_no = sb("tile_no", [P, 32])
        row_no = sb("row_no", [P, 1])
        bit, cand, sign, limit, kept, key = (sb(n, [P, E], U32) for n in ("bit", "cand", "sign", "limit", "kept", "key"))
        count = sb("count", [P, E])
        over = sb("over", wide, BF16)
        equal = sb("equal", wide, BF16)
        need = sb("need", [P, E])
        total = sb("total", wide)
        rank = sb("rank", wide)
        chosen = sb("chosen", wide, BF16)
        place = sb("place", wide)
        pmax, pneg = sb("pmax", [P, E]), sb("pneg", [P, E])
        grown = sb("grown", wide)
        gsum = sb("gsum", [P, E])
        onesf = sb("onesf", [P, P])
        place_hi, place_lo = sb("place_hi", wide), sb("place_lo", wide)
        A = [sb(f"A{n}", [P, NT, 32], BF16) for n in range(2)]
        C = [sb(f"C{n}", [P, NT, 2, 16], BF16) for n in range(2)]
        slot = sb("slot", [32, E, 16], U32)
        slotf = sb("slotf", [32, E, 2, 16])

        wq_n, wk_n = sb("wq_n", [P, KD, D]), sb("wk_n", [P, KD, D])
        wv_t = sb("wv_t", [P, KD, D])
        w_t, a1_n, a2_n = sb("w_t", [P, KD, D]), sb("a1_n", [P, KD, D]), sb("a2_n", [P, KD, D])
        wa_t = sb("wa_t", [P, KD, D])
        bq, bk = sb("bq", [P, KD]), sb("bk", [P, KD])
        bv = sb("bv", [1, D])
        bqb = sb("bqb", [P, KD, P])
        w2 = sb("w2", [P, KD])
        w2b = sb("w2b", [P, KD, P])
        u = sb("u", [P, KD])
        s0 = sb("s0", [P, 1])
        ctxt = [sb(f"ctxt{n}", [P, KD, J]) for n in range(2)]

        cnt_ps = [ps("cnt0"), ps("cnt1")]
        sum_ps = ps("sum")
        fold_ps = ps("fold")
        m_ps = [ps("m0"), ps("m1")]
        v_ps = [ps("v0"), ps("v1")]

        w_in = sem("w_in")
        consts, ones_set, zero_tri, tri_set, iota_set = sem("consts"), sem("ones_set"), sem("zero_tri"), sem("tri_set"), sem("iota_set")
        bit_set, cand_set, sign_set, limit_set = sem("bit_set"), sem("cand_set"), sem("sign_set"), sem("limit_set")
        over_set, counted, count_set, kept_set, key_set = sem("over_set"), sem("counted"), sem("count_set"), sem("kept_set"), sem("key_set")
        step_done, ranked = sem("step_done"), sem("ranked")
        max_set, max_all, grown_set = sem("max_set"), sem("max_all"), sem("grown_set")
        onehot, gathered, slot_set = sem("onehot"), sem("gathered"), sem("slot_set")
        slots_stored = sem("slots_stored")
        ctx_in = [sem(f"ctx_in{n}") for n in range(2)]
        folded, fold_read, bc_set = sem("folded"), sem("fold_read"), sem("bc_set")
        m_made, m_read, v_made, v_read = sem("m_made"), sem("m_read"), sem("v_made"), sem("v_read")

        block = ctx.enter_context(nc.Block())

        @block.sync
        def _(sp):
            for dst, name in ((wq_n, "wq1"), (wk_n, "wk1"), (wv_t, "wv1t"), (w_t, "ffwt"), (a1_n, "ffa1"), (a2_n, "ffa2")):
                sp.dma_start(dst[:, :, :], io[name]).then_inc(w_in, 16)
            sp.dma_start(bq[:, :], io["bq"]).then_inc(w_in, 16)
            sp.dma_start(bk[:, :], io["bk"]).then_inc(w_in, 16)
            sp.dma_start(bv[:, :], io["bv"].rearrange("(a c) -> a c", a=1)).then_inc(w_in, 16)
            for n in range(2):
                sp.dma_start(ctxt[n][:, :, :], io["ctxt"][n]).then_inc(ctx_in[n], 16)
            with sp.Fori(1, B // 2) as i:
                for c in range(2):
                    sp.wait_ge(v_made, 2 * i + (c - 1))
                    sp.dma_start(ctxt[c][:, :, :], io["ctxt"][2 * i + c]).then_inc(ctx_in[c], 16)
            sp.wait_ge(slot_set, E + 1)
            sp.dma_start(slots_dram.rearrange("e (a b) -> a e b", a=32), slot[:, :, :]).then_inc(slots_stored, 16)
            sp.wait_ge(slots_stored, 16)

        @block.gpsimd
        def _(pool):
            pool.memset(ones[:, :], 1.0).then_inc(ones_set, 1)
            pool.memset(onesf[:, :], 1.0).then_inc(ones_set, 1)
            pool.memset(tri[:, :], 0.0).then_inc(zero_tri, 1)
            pool.wait_ge(zero_tri, 1)
            pool.affine_select(out=tri[:, :], in_=tri[:, :], compare_op=ALU.is_gt, fill=1.0, base=0,
                               pattern=[[-1, P]], channel_multiplier=1).then_inc(tri_set, 1)
            pool.iota(iota[:, :], pattern=[[1, 32]], base=0, channel_multiplier=0).then_inc(iota_set, 1)
            pool.iota(row[:, :], pattern=[[0, 1]], base=0, channel_multiplier=1).then_inc(iota_set, 1)
            pool.wait_ge(max_set, 1)
            nc.gpsimd.partition_all_reduce(expert_max[:, :], pmax[:, :], P, bass.bass_isa.ReduceOp.max).then_inc(max_all, 1)

        @block.tensor
        def _(pe):
            pe.wait_ge(w_in, 16 * 9)
            folds = 0

            def fold(out_cols, pairs, signal=True):
                nonlocal folds
                if folds:
                    pe.wait_ge(fold_read, folds)
                folds += 1
                for out_ap, terms in pairs:
                    for n, (lhs, rhs) in enumerate(terms):
                        last = nc.tensor.matmul(out_ap, lhs, rhs, start=n == 0, stop=n == len(terms) - 1)
                last.then_inc(folded, 1)

            def cols(t):
                return slice(t * P, (t + 1) * P)

            fold(None, [(fold_ps[:, m * D:(m + 1) * D], [(wk_n[:, k, cols(m)], wq_n[:, k, :]) for k in range(KD)]) for m in range(KD)])
            fold(None, [(fold_ps[:, m * D:(m + 1) * D], [(a1_n[:, k, cols(m)], w_t[:, k, :]) for k in range(KD)]) for m in range(KD)])
            fold(None, [(fold_ps[:, m * D:(m + 1) * D], [(wa_t[:, k, cols(m)], a2_n[:, k, :]) for k in range(KD)]) for m in range(KD)])
            pe.wait_ge(bc_set, 1)
            fold(None, [(fold_ps[:, m:m + 1], [(wq_n[:, k, cols(m)], bk[:, k:k + 1]) for k in range(KD)]) for m in range(KD)]
                 + [(fold_ps[:, 2 + m:3 + m], [(wk_n[:, k, cols(m)], bq[:, k:k + 1]) for k in range(KD)]) for m in range(KD)]
                 + [(fold_ps[:, 4:5], [(bqb[:, k, :], bk[:, k:k + 1]) for k in range(KD)])])
            pe.wait_ge(fold_read, 3)
            pe.wait_ge(bc_set, 2)
            pe.wait_ge(ones_set, 2)

            def tally(n, c):
                pe.wait_ge(over_set, n + 1)
                nc.tensor.matmul(cnt_ps[c % 2][:, 0:E * NT], ones[:, :], over[:, :, :].rearrange("p e t -> p (e t)"),
                                 start=True, stop=True).then_inc(counted, 1)

            def second_keys(i, c):
                pe.wait_ge(ctx_in[c], 16 * (i + 1))
                if not (isinstance(i, int) and i == 0):
                    pe.wait_ge(m_read, 2 * i + (c - 1))
                for m in range(KD):
                    for k in range(KD):
                        nc.tensor.matmul(m_ps[c][:, m * J:(m + 1) * J], gt[:, k, cols(m)], ctxt[c][:, k, :],
                                         start=k == 0, stop=k == KD - 1)
                for k in range(KD):
                    last = nc.tensor.matmul(m_ps[c][:, 2 * J:3 * J], w2b[:, k, :], ctxt[c][:, k, :], start=k == 0, stop=k == KD - 1)
                last.then_inc(m_made, 1)

            def second_values(i, c):
                if not (isinstance(i, int) and i == 0):
                    pe.wait_ge(v_read, 2 * i + (c - 1))
                nc.tensor.matmul(v_ps[c][0:J, 0:D], onesf[0:1, 0:J], bv[0:1, :], start=True, stop=False)
                for k in range(KD):
                    last = nc.tensor.matmul(v_ps[c][0:J, 0:D], ctxt[c][:, k, :], wv_t[:, k, :], start=False, stop=k == KD - 1)
                last.then_inc(v_made, 1)

            def four_bits(i):
                for c in range(2):
                    tally(4 * i + 2 * c, 0)
                    second_keys(i, c)
                    tally(4 * i + (2 * c + 1), 1)
                    second_values(i, c)

            four_bits(0)
            with pe.Fori(1, B // 2) as i:
                four_bits(i)

            def prefix(n, src):
                pe.wait_ge(over_set, 32 + n)
                pe.wait_ge(tri_set, 1)
                nc.tensor.matmul(cnt_ps[1][:, 0:E * NT], ones[:, :], src, start=True, stop=True)
                nc.tensor.matmul(cnt_ps[0][:, 0:E * NT], tri[:, :], src, start=True, stop=True).then_inc(counted, 1)

            pe.wait_ge(over_set, 33)
            nc.tensor.matmul(sum_ps[:, 0:E * NT], ones[:, :], over[:, :, :].rearrange("p e t -> p (e t)"),
                             start=True, stop=True).then_inc(counted, 1)
            prefix(2, equal[:, :, :].rearrange("p e t -> p (e t)"))
            prefix(3, chosen[:, :, :].rearrange("p e t -> p (e t)"))
            pe.wait_ge(grown_set, 3)
            nc.tensor.matmul(sum_ps[:, 0:E], onesf[:, :], gsum[:, :], start=True, stop=True).then_inc(counted, 1)
            for e in range(E):
                pe.wait_ge(onehot, e + 1)
                if e >= 2:
                    pe.wait_ge(slot_set, e - 1)
                for t in range(NT):
                    last = nc.tensor.matmul(v_ps[e % 2][0:32, 0:32], A[e % 2][:, t, :],
                                            C[e % 2][:, t, :, :].rearrange("p a b -> p (a b)"), start=t == 0, stop=t == NT - 1)
                last.then_inc(gathered, 1)

        @block.scalar
        def _(act):
            for n, dst in enumerate((gt, wa_t, ffn_w)):
                act.wait_ge(folded, n + 1)
                nc.scalar.copy(dst[:, :, :].rearrange("p a b -> p (a b)"), fold_ps[:, :]).then_inc(fold_read, 1)
            act.wait_ge(bc_set, 2)

            def read(i, c):
                act.wait_ge(m_made, 2 * i + (c + 1))
                b = 2 * i + c
                for m in range(KD):
                    nc.scalar.activation(keys_m[:, bass.ds(KD * b + m, 1), :].rearrange("p a j -> p (a j)"), m_ps[c][:, m * J:(m + 1) * J], ACT.Identity, bias=u[:, m:m + 1])
                nc.scalar.activation(keys_bias[:, bass.ds(b, 1), :].rearrange("p a j -> p (a j)"), m_ps[c][:, 2 * J:3 * J], ACT.Identity, scale=D ** -0.5,
                                     bias=s0[:, 0:1]).then_inc(m_read, 1)
                act.wait_ge(v_made, 2 * i + (c + 1))
                nc.scalar.copy(values[:, bass.ds(b, 1), :].rearrange("p a j -> p (a j)"), v_ps[c][0:J, 0:D]).then_inc(v_read, 1)

            with act.Fori(0, B // 2) as i:
                for c in range(2):
                    read(i, c)
            act.wait_ge(grown_set, 1)
            nc.scalar.activation(grown[:, :, :], grown[:, :, :], ACT.Exp).then_inc(grown_set, 1)

        @block.vector
        def _(dve):
            V = nc.vector
            done = [0]

            def then(ins):
                done[0] += 1
                ins.then_inc(step_done, 1)
                dve.wait_ge(step_done, done[0])

            V.memset(keep[:, :, :], 1.0).then_inc(consts, 1)
            dve.wait_ge(consts, 1)
            V.memset(keep[:, :, 0:1], 0.0).then_inc(consts, 1)
            V.memset(bit[:, :], 1).then_inc(consts, 1)
            V.memset(key[:, :], 0).then_inc(key_set, 1)
            dve.wait_ge(iota_set, 2)
            V.tensor_copy(tile_no[:, :], iota[:, :]).then_inc(consts, 1)
            V.tensor_copy(row_no[:, :], row[:, :]).then_inc(consts, 1)
            dve.wait_ge(consts, 5)
            V.tensor_scalar(bit[:, :], bit[:, :], 31, None, ALU.logical_shift_left).then_inc(bit_set, 1)
            V.tensor_reduce(pmax[:, :], scores[:, :, :], AX.X, ALU.max).then_inc(max_set, 1)
            dve.wait_ge(w_in, 16 * 9)
            V.tensor_copy(bqb[:, :, :], bq[:, :].unsqueeze(2).to_broadcast([P, KD, P])).then_inc(bc_set, 1)
            dve.wait_ge(folded, 4)
            then(V.tensor_copy(u[:, :], fold_ps[:, 0:2]))
            then(V.tensor_scalar(s0[:, :], fold_ps[:, 4:5], D ** -0.5, None, ALU.mult))
            then(V.tensor_copy(w2[:, :], fold_ps[:, 2:4]))
            V.tensor_copy(w2b[:, :, :], w2[:, :].unsqueeze(2).to_broadcast([P, KD, P])).then_inc(bc_set, 1)

            def one_bit(n, c):
                dve.wait_ge(key_set, n + 1)
                dve.wait_ge(bit_set, n + 1)
                V.tensor_tensor(cand[:, :], key[:, :], bit[:, :], ALU.bitwise_or).then_inc(cand_set, 1)
                dve.wait_ge(cand_set, n + 1)
                V.tensor_scalar(sign[:, :], cand[:, :], 31, 0xFFFFFFFF, ALU.arith_shift_right, ALU.bitwise_xor).then_inc(sign_set, 1)
                dve.wait_ge(sign_set, n + 1)
                V.scalar_tensor_tensor(out=limit[:, :], in0=sign[:, :], scalar=0x80000000, in1=cand[:, :],
                                       op0=ALU.bitwise_or, op1=ALU.bitwise_xor).then_inc(limit_set, 1)
                dve.wait_ge(limit_set, n + 1)
                V.tensor_tensor(over[:, :, :], scores[:, :, :], limit[:, :].bitcast(F32).unsqueeze(2).to_broadcast(wide),
                                ALU.is_ge).then_inc(over_set, 1)
                dve.wait_ge(counted, n + 1)
                V.tensor_reduce(count[:, :], cnt_ps[c][:, 0:E * NT].rearrange("p (e t) -> p e t", e=E), AX.X, ALU.add).then_inc(count_set, 1)
                dve.wait_ge(count_set, n + 1)
                V.scalar_tensor_tensor(out=kept[:, :], in0=count[:, :], scalar=CAP - 0.5, in1=bit[:, :],
                                       op0=ALU.is_gt, op1=ALU.mult).then_inc(kept_set, 1)
                dve.wait_ge(kept_set, n + 1)
                V.tensor_tensor(key[:, :], key[:, :], kept[:, :], ALU.bitwise_or).then_inc(key_set, 1)
                V.tensor_scalar(bit[:, :], bit[:, :], 1, None, ALU.logical_shift_right).then_inc(bit_set, 1)

            with dve.Fori(0, 8) as i:
                for c in range(4):
                    one_bit(4 * i + c, c % 2)

            dve.wait_ge(key_set, 33)
            then(V.tensor_scalar(sign[:, :], key[:, :], 31, 0xFFFFFFFF, ALU.arith_shift_right, ALU.bitwise_xor))
            then(V.scalar_tensor_tensor(out=limit[:, :], in0=sign[:, :], scalar=0x80000000, in1=key[:, :],
                                        op0=ALU.bitwise_or, op1=ALU.bitwise_xor))
            least = limit[:, :].bitcast(F32).unsqueeze(2).to_broadcast(wide)
            V.tensor_tensor(over[:, :, :], scores[:, :, :], least, ALU.is_gt).then_inc(over_set, 1)
            V.tensor_tensor(equal[:, :, :], scores[:, :, :], least, ALU.is_equal).then_inc(over_set, 1)
            dve.wait_ge(counted, 33)
            then(V.tensor_reduce(count[:, :], sum_ps[:, 0:E * NT].rearrange("p (e t) -> p e t", e=E), AX.X, ALU.add))
            then(V.tensor_scalar(need[:, :], count[:, :], -1.0, float(CAP), ALU.mult, ALU.add))

            def up_to(dst):
                then(V.tensor_copy(total[:, :, :].rearrange("p e t -> p (e t)"), cnt_ps[1][:, 0:E * NT]))
                then(V.tensor_tensor_scan(dst[:, :, :].rearrange("p e t -> p (e t)"), keep[:, :, :].rearrange("p e t -> p (e t)"),
                                          total[:, :, :].rearrange("p e t -> p (e t)"), 0.0, ALU.mult, ALU.add))
                then(V.tensor_tensor(dst[:, :, :], dst[:, :, :], total[:, :, :], ALU.subtract))
                then(V.tensor_tensor(dst[:, :, :].rearrange("p e t -> p (e t)"), cnt_ps[0][:, 0:E * NT],
                                     dst[:, :, :].rearrange("p e t -> p (e t)"), ALU.add))

            dve.wait_ge(counted, 34)
            up_to(rank)
            then(V.tensor_tensor(rank[:, :, :], rank[:, :, :], need[:, :].unsqueeze(2).to_broadcast(wide), ALU.is_le))
            then(V.tensor_tensor(rank[:, :, :], rank[:, :, :], equal[:, :, :], ALU.mult))
            V.tensor_tensor(chosen[:, :, :], rank[:, :, :], over[:, :, :], ALU.add).then_inc(over_set, 1)
            dve.wait_ge(max_all, 1)
            V.tensor_tensor(grown[:, :, :], scores[:, :, :], expert_max[:, :].unsqueeze(2).to_broadcast(wide),
                            ALU.subtract).then_inc(grown_set, 1)
            dve.wait_ge(counted, 35)
            up_to(place)
            then(V.tensor_tensor(place[:, :, :], place[:, :, :], chosen[:, :, :], ALU.mult))
            then(V.tensor_scalar(place[:, :, :], place[:, :, :], -1.0, None, ALU.add))
            then(V.tensor_copy(total[:, :, :].bitcast(I32), place[:, :, :]))
            V.tensor_scalar(place_lo[:, :, :].bitcast(I32), total[:, :, :].bitcast(I32), 15, None, ALU.bitwise_and).then_inc(ranked, 1)
            V.tensor_scalar(place_hi[:, :, :].bitcast(I32), total[:, :, :].bitcast(I32), 4, None, ALU.arith_shift_right).then_inc(ranked, 1)
            dve.wait_ge(ranked, 2)
            V.tensor_copy(rank[:, :, :], place_lo[:, :, :].bitcast(I32)).then_inc(ranked, 1)
            V.tensor_copy(place[:, :, :], place_hi[:, :, :].bitcast(I32)).then_inc(ranked, 1)
            dve.wait_ge(grown_set, 2)
            then(V.tensor_tensor(grown[:, :, :], grown[:, :, :], chosen[:, :, :], ALU.mult))
            V.tensor_reduce(gsum[:, :], grown[:, :, :], AX.X, ALU.add).then_inc(grown_set, 1)
            dve.wait_ge(counted, 36)
            then(V.tensor_copy(count[:, :], sum_ps[:, 0:E]))
            V.reciprocal(expert_inv[:, :], count[:, :])
            dve.wait_ge(ranked, 4)

            def read_slots(e):
                dve.wait_ge(gathered, e + 1)
                V.tensor_copy(slotf[:, e, :, :].rearrange("p a b -> p (a b)"), v_ps[e % 2][0:32, 0:32]).then_inc(slot_set, 1)

            for e in range(E):
                if e >= 2:
                    dve.wait_ge(gathered, e - 1)
                then(V.tensor_tensor(A[e % 2][:, :, :], place[:, e, :].unsqueeze(2).to_broadcast([P, NT, 32]),
                                     tile_no[:, :].unsqueeze(1).to_broadcast([P, NT, 32]), ALU.is_equal))
                then(V.tensor_tensor(C[e % 2][:, :, 1, :], rank[:, e, :].unsqueeze(2).to_broadcast([P, NT, 16]),
                                     tile_no[:, 0:16].unsqueeze(1).to_broadcast([P, NT, 16]), ALU.is_equal))
                then(V.tensor_tensor(C[e % 2][:, :, 0, :], C[e % 2][:, :, 1, :],
                                     tile_no[:, :].unsqueeze(2).to_broadcast([P, NT, 16]), ALU.mult))
                V.tensor_scalar(C[e % 2][:, :, 1, :], C[e % 2][:, :, 1, :], row_no[:, 0:1], None, ALU.mult).then_inc(onehot, 1)
                if e >= 1:
                    read_slots(e - 1)
            read_slots(E - 1)
            dve.wait_ge(slot_set, E)
            V.scalar_tensor_tensor(out=slot[:, :, :], in0=slotf[:, :, 0, :], scalar=float(P), in1=slotf[:, :, 1, :],
                                   op0=ALU.mult, op1=ALU.add).then_inc(slot_set, 1)


def expert_loop(eng, body):
    for c in range(2):
        body(0, c)
    with eng.Fori(1, E // 2 - 1) as i:
        for c in range(2):
            body(i, c)
    for c in range(2):
        body(E // 2 - 1, c)


def experts(nc, io, x1_dram, xn1_dram, slots_dram, ident, expert_max, expert_inv):
    QT = CAP // P
    HT = HID // P
    with ExitStack() as ctx:
        def sb(name, shape, dt=F32):
            return ctx.enter_context(nc.sbuf_tensor("e_" + name, shape, dt))

        def ps(name):
            return ctx.enter_context(nc.psum_tensor("ep_" + name, [P, 512], F32))

        def sem(name):
            return ctx.enter_context(nc.semaphore("e_" + name))

        wraw = [sb(f"wraw{n}", [P, 3, KD * HID]) for n in range(2)]
        wh = [sb(f"wh{n}", [P, 3, KD * HID], F32R) for n in range(2)]
        wl = [sb(f"wl{n}", [P, 3, KD * HID], F32R) for n in range(2)]
        wg = sb("wg", [P, E, D])
        slots = sb("slots", [P, E, QT], U32)
        xg = [sb(f"xg{n}", [P, QT, D]) for n in range(2)]
        xgh = sb("xgh", [P, KD, CAP], F32R)
        xgl = sb("xgl", [P, KD, CAP], F32R)
        prod = sb("prod", [P, D])
        gate = [sb(f"gate{n}", [P, QT]) for n in range(2)]
        weight = [sb(f"weight{n}", [P, QT]) for n in range(2)]
        negmax = sb("negmax", [P, E])
        halfinv = sb("halfinv", [P, E])
        th = [sb(f"th{n}", [P, CAP]) for n in range(2)]
        gated = [sb(f"gated{n}", [P, CAP]) for n in range(2)]
        hid = [sb(f"hid{n}", [P, CAP]) for n in range(2)]
        hh = sb("hh", [P, HT, CAP], F32R)
        hl = sb("hl", [P, HT, CAP], F32R)
        y = [sb(f"y{n}", [P, QT, D]) for n in range(2)]

        t_ps = [ps("t0"), ps("t1")]
        u_ps = [ps("u0"), ps("u1")]
        g_ps = [ps("g0"), ps("g1")]
        y_ps = [ps("y0"), ps("y1")]

        small_in, slots_in = sem("small_in"), sem("slots_in")
        w_in = [sem(f"w_in{n}") for n in range(2)]
        w_hi, w_lo = sem("w_hi"), sem("w_lo")
        x_in = [sem(f"x_in{n}") for n in range(2)]
        added = [sem(f"added{n}") for n in range(2)]
        signs, products, gates_done, exped, weighted = sem("signs"), sem("products"), sem("gates_done"), sem("exped"), sem("weighted")
        t_made, t_hi, t_lo = sem("t_made"), sem("t_hi"), sem("t_lo")
        up_made, tanh_done, gated_done, hid_done, h_hi, h_lo = (sem(n) for n in ("up_made", "tanh_done", "gated_done", "hid_done", "h_hi", "h_lo"))
        y_made, y_done = sem("y_made"), sem("y_done")

        block = ctx.enter_context(nc.Block())

        @block.sync
        def _(sp):
            sp.dma_start(slots[:, :, :], slots_dram.rearrange("e (p q) -> p e q", p=P)).then_inc(slots_in, 16)
            sp.dma_start(wg[:, :, :].rearrange("p e c -> p (e c)"), io["wg"].rearrange("(a e) c -> a (e c)", a=1).to_broadcast([P, E * D])).then_inc(small_in, 16)

            def load(i, c):
                sp.dma_start(wraw[c][:, :, :], io["we"][2 * i + c]).then_inc(w_in[c], 16)

            load(0, 0)
            load(0, 1)
            with sp.Fori(1, E // 2) as i:
                for c in range(2):
                    sp.wait_ge(w_lo, 2 * i + (c - 1))
                    load(i, c)

        @block.gpsimd
        def _(pool):
            def gather(i, c):
                e = 2 * i + c
                for q in range(QT):
                    pool.indirect_dma_start(out=xg[c][:, q, :], out_offset=None, in_=xn1_dram,
                                            in_offset=bass.IndirectOffsetOnAxis(ap=slots[:, e, q:q + 1], axis=0)).then_inc(x_in[c], 16)

            def scatter(i, c):
                e = 2 * i + c
                pool.wait_ge(y_done, e + 1)
                for q in range(QT):
                    pool.indirect_dma_start(out=x1_dram, out_offset=bass.IndirectOffsetOnAxis(ap=slots[:, e, q:q + 1], axis=0),
                                            in_=y[c][:, q, :], in_offset=None, compute_op=ALU.add).then_inc(added[c], 16)

            pool.wait_ge(slots_in, 16)
            gather(0, 0)
            gather(0, 1)
            for i in range(E // 2):
                for c in range(2):
                    e = 2 * i + c
                    if e + 2 < E:
                        pool.wait_ge(t_made, 2 * (e + 1))
                        pool.wait_ge(gates_done, e + 1)
                        gather(i + 1, c)
                    if e >= 1:
                        pool.wait_ge(added[1 - c], 16 * QT * ((e - 1) // 2 + 1))
                    scatter(i, c)
            pool.wait_ge(added[1], 16 * QT * (E // 2))

        @block.tensor
        def _(pe):
            def mm3(out_ap, lhs, rhs, start, stop):
                (lh, ll), (rh, rl) = lhs, rhs
                nc.tensor.matmul(out_ap, lh, rh, start=start, stop=False)
                nc.tensor.matmul(out_ap, lh, rl, start=False, stop=False)
                return nc.tensor.matmul(out_ap, ll, rh, start=False, stop=stop)

            def turn(i, c):
                e = 2 * i + c
                pe.wait_ge(x_in[c], 16 * QT * (i + 1))
                for k in range(KD):
                    if not (isinstance(e, int) and e == 0):
                        pe.wait_ge(t_lo, 2 * e - 1 + k)
                    for q in range(QT):
                        last = nc.tensor.transpose(t_ps[k][:, q * P:(q + 1) * P], xg[c][:, q, k * P:(k + 1) * P], ident[:, :])
                    last.then_inc(t_made, 1)

            def up(i, c):
                e = 2 * i + c
                pe.wait_ge(t_hi, 2 * e + 2)
                pe.wait_ge(t_lo, 2 * e + 2)
                pe.wait_ge(w_hi, e + 1)
                pe.wait_ge(w_lo, e + 1)
                for m in range(HT):
                    if not (isinstance(e, int) and e == 0 and m < 2):
                        pe.wait_ge(hid_done, HT * e + m - 1)
                    for bank, w in ((u_ps[m % 2], 0), (g_ps[m % 2], 1)):
                        for k in range(KD):
                            cols = slice(k * HID + m * P, k * HID + (m + 1) * P)
                            last = mm3(bank[:, :], (wh[c][:, w, cols], wl[c][:, w, cols]), (xgh[:, k, :], xgl[:, k, :]),
                                       k == 0, k == KD - 1)
                        last.then_inc(up_made, 1)

            def down(i, c):
                e = 2 * i + c
                pe.wait_ge(h_hi, HT * (e + 1))
                pe.wait_ge(h_lo, HT * (e + 1))
                for q in range(QT):
                    if not (isinstance(e, int) and e == 0) and q % 2 == 0:
                        pe.wait_ge(y_done, e)
                    for m in range(HT):
                        rows, cols = slice(q * P, (q + 1) * P), slice(m * D, (m + 1) * D)
                        last = mm3(y_ps[q // 2][:, (q % 2) * D:(q % 2 + 1) * D], (hh[:, m, rows], hl[:, m, rows]),
                                   (wh[c][:, 2, cols], wl[c][:, 2, cols]), m == 0, m == HT - 1)
                    if q % 2:
                        last.then_inc(y_made, 1)

            turn(0, 0)

            def body(i, c):
                up(i, c)
                if c == 0:
                    turn(i, 1)
                elif not (isinstance(i, int) and i == E // 2 - 1):
                    turn(i + 1, 0)
                down(i, c)

            expert_loop(pe, body)

        @block.scalar
        def _(act):
            def split_weights(i, c):
                e = 2 * i + c
                act.wait_ge(w_in[c], 16 * (i + 1))
                if not (isinstance(i, int) and i == 0):
                    act.wait_ge(y_made, 2 * e - 2)
                nc.scalar.copy(wh[c][:, :, :], wraw[c][:, :, :]).then_inc(w_hi, 1)

            def leading(i, c):
                e = 2 * i + c
                for k in range(KD):
                    act.wait_ge(t_made, 2 * e + k + 1)
                    if not (isinstance(e, int) and e == 0) and k == 0:
                        act.wait_ge(up_made, 2 * HT * e)
                    nc.scalar.copy(xgh[:, k, :], t_ps[k][:, :]).then_inc(t_hi, 1)

            act.wait_ge(small_in, 16)
            leading(0, 0)
            split_weights(0, 0)
            split_weights(0, 1)

            def body(i, c):
                e = 2 * i + c
                act.wait_ge(gates_done, e + 1)
                nc.scalar.activation(weight[c][:, :], gate[c][:, :], ACT.Exp, bias=negmax[:, bass.ds(e, 1)]).then_inc(exped, 1)
                for m in range(HT):
                    act.wait_ge(up_made, 2 * HT * e + (2 * m + 1))
                    if not (isinstance(e, int) and e == 0 and m < 2):
                        act.wait_ge(gated_done, HT * e + (m - 1))
                    nc.scalar.activation(th[m % 2][:, :], u_ps[m % 2][:, :], ACT.Tanh, scale=0.5).then_inc(tanh_done, 1)
                    act.wait_ge(hid_done, HT * e + (m + 1))
                    if not (isinstance(e, int) and e == 0) and m == 0:
                        act.wait_ge(y_made, 2 * e)
                    nc.scalar.copy(hh[:, m, :], hid[m % 2][:, :]).then_inc(h_hi, 1)
                if c == 0:
                    leading(i, 1)
                elif not (isinstance(i, int) and i == E // 2 - 1):
                    leading(i + 1, 0)
                act.wait_ge(weighted, e + 1)
                if not (isinstance(i, int) and i == 0):
                    act.wait_ge(added[c], 16 * QT * i)
                for n in range(2):
                    act.wait_ge(y_made, 2 * e + (n + 1))
                    for q in (2 * n, 2 * n + 1):
                        last = nc.scalar.mul(y[c][:, q, :], y_ps[n][:, (q % 2) * D:(q % 2 + 1) * D], weight[c][:, q:q + 1])
                last.then_inc(y_done, 1)
                if not (isinstance(i, int) and i == E // 2 - 1):
                    split_weights(i + 1, c)

            expert_loop(act, body)

        @block.vector
        def _(dve):
            V = nc.vector
            V.tensor_scalar(negmax[:, :], expert_max[:, :], -1.0, None, ALU.mult).then_inc(signs, 1)
            V.tensor_scalar(halfinv[:, :], expert_inv[:, :], 0.5, None, ALU.mult).then_inc(signs, 1)
            dve.wait_ge(small_in, 16)
            dve.wait_ge(signs, 2)

            def score(i, c):
                e = 2 * i + c
                dve.wait_ge(x_in[c], 16 * QT * (i + 1))
                if not (isinstance(i, int) and i == 0):
                    dve.wait_ge(exped, e - 1)
                for q in range(QT):
                    dve.wait_ge(products, QT * e + q) if not (isinstance(e, int) and e == 0 and q == 0) else None
                    V.tensor_tensor(prod[:, :], xg[c][:, q, :], wg[:, bass.ds(e, 1), :].rearrange("p a c -> p (a c)"), ALU.mult).then_inc(signs, 1)
                    dve.wait_ge(signs, QT * e + (q + 3))
                    V.tensor_reduce(gate[c][:, q:q + 1], prod[:, :], AX.X, ALU.add).then_inc(products, 1)
                dve.wait_ge(products, QT * (e + 1))
                V.tensor_copy(gate[c][:, :], gate[c][:, :]).then_inc(gates_done, 1)

            def rest(i, c):
                e = 2 * i + c
                for k in range(KD):
                    dve.wait_ge(t_hi, 2 * e + (k + 1))
                    V.tensor_tensor(xgl[:, k, :], t_ps[k][:, :], xgh[:, k, :].bitcast(F32), ALU.subtract).then_inc(t_lo, 1)

            def split_weights(i, c):
                dve.wait_ge(w_hi, 2 * i + (c + 1))
                V.tensor_tensor(wl[c][:, :, :], wraw[c][:, :, :], wh[c][:, :, :].bitcast(F32), ALU.subtract).then_inc(w_lo, 1)

            rest(0, 0)
            split_weights(0, 0)
            score(0, 0)

            def body(i, c):
                e = 2 * i + c
                dve.wait_ge(exped, e + 1)
                V.tensor_scalar(weight[c][:, :], weight[c][:, :], halfinv[:, bass.ds(e, 1)], None, ALU.mult).then_inc(weighted, 1)
                for m in range(HT):
                    dve.wait_ge(tanh_done, HT * e + (m + 1))
                    V.scalar_tensor_tensor(out=gated[m % 2][:, :], in0=th[m % 2][:, :], scalar=1.0, in1=u_ps[m % 2][:, :],
                                           op0=ALU.add, op1=ALU.mult).then_inc(gated_done, 1)
                    dve.wait_ge(gated_done, HT * e + (m + 1))
                    dve.wait_ge(up_made, 2 * HT * e + (2 * m + 2))
                    if not (isinstance(e, int) and e == 0 and m < 2):
                        dve.wait_ge(h_lo, HT * e + (m - 1))
                        dve.wait_ge(h_hi, HT * e + (m - 1))
                    V.tensor_tensor(hid[m % 2][:, :], gated[m % 2][:, :], g_ps[m % 2][:, :], ALU.mult).then_inc(hid_done, 1)
                    dve.wait_ge(h_hi, HT * e + (m + 1))
                    V.tensor_tensor(hl[:, m, :], hid[m % 2][:, :], hh[:, m, :].bitcast(F32), ALU.subtract).then_inc(h_lo, 1)
                if c == 0:
                    rest(i, 1)
                    split_weights(i, 1)
                    score(i, 1)
                elif not (isinstance(i, int) and i == E // 2 - 1):
                    rest(i + 1, 0)
                    split_weights(i + 1, 0)
                    score(i + 1, 0)

            expert_loop(dve, body)


def second_layer(nc, io, x2_dram, out_dram, ident, second):
    _, keys_m, keys_bias, values, ffn_w = second
    SC = D ** -0.5
    with ExitStack() as ctx:
        def sb(name, shape, dt=F32):
            return ctx.enter_context(nc.sbuf_tensor("l_" + name, shape, dt))

        def ps(name):
            return ctx.enter_context(nc.psum_tensor("lp_" + name, [P, 512], F32))

        sems = []

        def sem(name):
            sems.append(ctx.enter_context(nc.semaphore("l_" + name)))
            return sems[-1]

        x2 = [sb(f"x2{n}", [P, TT, D]) for n in range(4)]
        side = [sb(f"side{n}", [P, TT, J]) for n in range(2)]
        betas = sb("betas", [P, 3])
        coef = sb("coef", [P, 1])
        neghalf = sb("neghalf", [P, TT])
        bias_w = sb("bias_w", [P, D])
        sided = [sb(f"sided{n}", [P, TT, J]) for n in range(2)]
        bn = [sb(f"bn{n}", [P, TT, 6]) for n in range(2)]
        turnstile = sb("turnstile", [P, 1])
        mv = [sb(f"mv{n}", [P, TT, 2]) for n in range(2)]
        var = [sb(f"var{n}", [P, TT]) for n in range(2)]
        rstd = [sb(f"rstd{n}", [P, TT]) for n in range(2)]
        xn = [sb(f"xn{n}", [P, TT, D]) for n in range(2)]
        xt = [sb(f"xt{n}", [P, KD, S]) for n in range(2)]
        att = [sb(f"att{n}", [P, TT, J]) for n in range(2)]
        negmax = sb("negmax", [P, TT])
        den = sb("den", [P, TT])
        rden = sb("rden", [P, TT])
        pt = sb("pt", [J, S])
        x3 = [sb(f"x3{n}", [P, TT, D]) for n in range(4)]
        pre = sb("pre", [P, TT, D])
        res = [sb(f"res{n}", [P, TT, D]) for n in range(2)]

        xt_ps = [ps("xt0"), ps("xt1")]
        sim_ps, pt_ps, pv_ps, ff_ps = ps("sim"), ps("pt"), ps("pv"), ps("ff")

        small_in = sem("small_in")
        x_in = [sem(f"x_in{n}") for n in range(4)]
        side_in = [sem(f"side_in{n}") for n in range(2)]
        pre_set = sem("pre_set")
        coef_set, sided_a, sided_b = sem("coef_set"), sem("sided_a"), sem("sided_b")
        bn_done = [sem("bn0"), sem("bn1")]
        mv_done = [sem("mv0"), sem("mv1")]
        var_done = [sem("var0"), sem("var1")]
        rstd_done = [sem("rstd0"), sem("rstd1")]
        xn_done = [sem("xn0"), sem("xn1")]
        xt_made = [sem("xt_made0"), sem("xt_made1")]
        xt_out = [sem("xt_out0"), sem("xt_out1")]
        sim_made, att_done, max_done, exped, inverted = sem("sim_made"), sem("att_done"), sem("max_done"), sem("exped"), sem("inverted")
        pt_made, pt_out, pv_made, x3_done = sem("pt_made"), sem("pt_out"), sem("pv_made"), sem("x3_done")
        ff_made, pre_done, tanh_done, res_done = sem("ff_made"), sem("pre_done"), sem("tanh_done"), sem("res_done")
        stored = [sem(f"stored{n}") for n in range(2)]

        x2_view = x2_dram.rearrange("(b t p) c -> b p t c", p=P, t=TT)
        out_view = out_dram.rearrange("b (t p) c -> b p t c", p=P)
        side_view = io["fside"].rearrange("b (t p) j -> b p t j", p=P)
        flat = "p a b -> p (a b)"

        def loop(eng, body, lags):
            for n in range(8):
                body(Batch4(0, n))
            with eng.Fori(2, B // 4) as i:
                for c in range(4):
                    body(Batch4(i, c))
            for n in range(B, B + lags):
                body(Batch4(0, n))

        clear_semaphores(nc, sems)
        block = ctx.enter_context(nc.Block())
        LAGS = 5

        @block.sync
        def _(sp):
            sp.dma_start(betas[:, :], io["betas"].unsqueeze(0).to_broadcast([P, 3])).then_inc(small_in, 16)
            sp.dma_start(bias_w[:, :], io["ffb"].unsqueeze(0).to_broadcast([P, D])).then_inc(small_in, 16)

            def loads(b):
                if b.at_least(4):
                    sp.wait_ge(x3_done, b.n - 3)
                sp.dma_start(x2[b.c % 4][:, :, :], x2_view[b.n]).then_inc(x_in[b.c % 4], 16)
                if b.at_least(2):
                    sp.wait_ge(sided_a, b.n - 1)
                sp.dma_start(side[b.c % 2][:, :, :], side_view[b.n]).then_inc(side_in[b.c % 2], 16)

            def body(n):
                if n.real():
                    loads(n)
                b = n.shift(-5)
                if b.real():
                    sp.wait_ge(res_done, b.n + 1)
                    sp.dma_start(out_view[b.n], res[b.c % 2][:, :, :]).then_inc(stored[b.c % 2], 16)

            loop(sp, body, LAGS)
            for n in range(2):
                sp.wait_ge(stored[n], 16 * (B // 2))

        @block.tensor
        def _(pe):
            def transposes(which, b):
                pe.wait_ge(xn_done[which], b.n + 1)
                if b.at_least(1):
                    pe.wait_ge(xt_out[which], b.n)
                for t in range(TT):
                    for k in range(KD):
                        last = nc.tensor.transpose(xt_ps[which][:, k * S + t * P:k * S + (t + 1) * P],
                                                   xn[which][:, t, k * P:(k + 1) * P], ident[:, :])
                last.then_inc(xt_made[which], 1)

            def scores(b):
                pe.wait_ge(xt_out[0], b.n + 1)
                if b.at_least(1):
                    pe.wait_ge(att_done, b.n)
                for t in range(TT):
                    for k in range(KD):
                        last = nc.tensor.matmul(sim_ps[:, t * J:(t + 1) * J], xt[0][:, k, t * P:(t + 1) * P],
                                                keys_m[:, bass.ds(KD * b.n + k, 1), :].rearrange("p a j -> p (a j)"), start=k == 0, stop=k == KD - 1)
                last.then_inc(sim_made, 1)

            def attention(b):
                pe.wait_ge(exped, b.n + 1)
                if b.at_least(1):
                    pe.wait_ge(pt_out, b.n)
                for t in range(TT):
                    last = nc.tensor.transpose(pt_ps[0:J, t * P:(t + 1) * P], att[b.c % 2][:, t, :], ident[:, :])
                last.then_inc(pt_made, 1)

            def mix(b):
                pe.wait_ge(pt_out, b.n + 1)
                if b.at_least(1):
                    pe.wait_ge(x3_done, b.n)
                for t in range(TT):
                    last = nc.tensor.matmul(pv_ps[:, t * D:(t + 1) * D], pt[:, t * P:(t + 1) * P],
                                            values[:, bass.ds(b.n, 1), :].rearrange("p a c -> p (a c)"), start=True, stop=True)
                last.then_inc(pv_made, 1)

            def feed(b):
                pe.wait_ge(xt_out[1], b.n + 1)
                if b.at_least(1):
                    pe.wait_ge(pre_done, b.n)
                for t in range(TT):
                    for k in range(KD):
                        last = nc.tensor.matmul(ff_ps[:, t * D:(t + 1) * D], xt[1][:, k, t * P:(t + 1) * P], ffn_w[:, k, :],
                                                start=k == 0, stop=k == KD - 1)
                last.then_inc(ff_made, 1)

            def body(n):
                if n.shift(-2).real():
                    scores(n.shift(-2))
                if n.shift(-3).real():
                    attention(n.shift(-3))
                if n.shift(-5).real():
                    feed(n.shift(-5))
                if n.shift(-4).real():
                    transposes(1, n.shift(-4))
                if n.shift(-1).real():
                    transposes(0, n.shift(-1))
                if n.shift(-3).real():
                    mix(n.shift(-3))

            loop(pe, body, LAGS)

        @block.scalar
        def _(act):
            act.wait_ge(coef_set, 2)

            def sides(b):
                act.wait_ge(side_in[b.c % 2], 16 * (b.turn(2) + 1))
                if b.at_least(2):
                    act.wait_ge(att_done, b.n - 1)
                nc.scalar.mul(sided[b.c % 2][:, :, :], side[b.c % 2][:, :, :], coef[:, 0:1]).then_inc(sided_a, 1)

            def xt_copy(which, b):
                act.wait_ge(xt_made[which], b.n + 1)
                if b.at_least(1):
                    act.wait_ge(sim_made if which == 0 else ff_made, b.n)
                nc.scalar.copy(xt[which][:, :, :].rearrange(flat), xt_ps[which][:, :]).then_inc(xt_out[which], 1)

            def exps(b):
                act.wait_ge(max_done, b.n + 1)
                if b.at_least(1):
                    act.wait_ge(inverted, b.n)
                for t in range(TT):
                    last = nc.scalar.activation(att[b.c % 2][:, t, :], att[b.c % 2][:, t, :], ACT.Exp, bias=negmax[:, t:t + 1],
                                                accum_out=den[:, t:t + 1])
                last.then_inc(exped, 1)

            def pt_copy(b):
                act.wait_ge(pt_made, b.n + 1)
                if b.at_least(1):
                    act.wait_ge(pv_made, b.n)
                nc.scalar.copy(pt[:, :], pt_ps[0:J, 0:S]).then_inc(pt_out, 1)

            def tanh(b):
                act.wait_ge(pre_done, b.n + 1)
                nc.scalar.activation(pre[:, :, :], pre[:, :, :], ACT.Tanh).then_inc(tanh_done, 1)

            def body(n):
                if n.shift(-3).real():
                    pt_copy(n.shift(-3))
                if n.shift(-4).real():
                    xt_copy(1, n.shift(-4))
                if n.shift(-1).real():
                    xt_copy(0, n.shift(-1))
                if n.shift(-2).real():
                    exps(n.shift(-2))
                if n.shift(-5).real():
                    tanh(n.shift(-5))
                if n.real():
                    sides(n)

            loop(act, body, LAGS)

        @block.gpsimd
        def _(pool):
            pool.memset(neghalf[:, :], -0.5).then_inc(coef_set, 1)
            pool.wait_ge(coef_set, 1)

            def rsqrt(which, b):
                pool.wait_ge(var_done[which], b.n + 1)
                nc.gpsimd.tensor_tensor(rstd[which][:, :], var[which][:, :], neghalf[:, :], ALU.pow).then_inc(rstd_done[which], 1)

            def add_keys(b):
                pool.wait_ge(sided_a, b.n + 1)
                nc.gpsimd.tensor_tensor(sided[b.c % 2][:, :, :], sided[b.c % 2][:, :, :],
                                        keys_bias[:, bass.ds(b.n, 1), :].to_broadcast([P, TT, J]), ALU.add).then_inc(sided_b, 1)

            def finish(b):
                pool.wait_ge(tanh_done, b.n + 1)
                if b.at_least(2):
                    pool.wait_ge(stored[b.c % 2], 16 * b.turn(2))
                nc.gpsimd.tensor_tensor(res[b.c % 2][:, :, :], pre[:, :, :], x3[b.c % 4][:, :, :], ALU.add).then_inc(res_done, 1)

            def body(n):
                if n.shift(-5).real():
                    finish(n.shift(-5))
                if n.shift(-3).real():
                    rsqrt(1, n.shift(-3))
                if n.real():
                    rsqrt(0, n)
                    add_keys(n)

            loop(pool, body, LAGS)

        @block.vector
        def _(dve):
            V = nc.vector
            dve.wait_ge(small_in, 32)
            V.tensor_tensor(coef[:, :], betas[:, 0:1], betas[:, 1:2], ALU.add).then_inc(pre_set, 1)
            dve.wait_ge(pre_set, 1)
            dve.wait_ge(coef_set, 1)
            V.tensor_tensor(coef[:, :], coef[:, :], betas[:, 2:3], ALU.subtract).then_inc(coef_set, 1)

            def statistics(which, b, src):
                for t in range(TT):
                    last = V.bn_stats(bn[which][:, t, :], src[:, t, :])
                last.then_inc(bn_done[which], 1)
                dve.wait_ge(bn_done[which], b.n + 1)
                V.memset(turnstile[:, :], 0.0)
                for t in range(TT):
                    last = V.bn_aggr(mv[which][:, t, :], bn[which][:, t, :])
                last.then_inc(mv_done[which], 1)
                dve.wait_ge(mv_done[which], b.n + 1)
                V.tensor_scalar(var[which][:, :], mv[which][:, :, 1], EPS, None, ALU.add).then_inc(var_done[which], 1)

            def normal(which, b, src):
                dve.wait_ge(rstd_done[which], b.n + 1)
                if b.at_least(1):
                    dve.wait_ge(xt_made[which], b.n)
                for t in range(TT):
                    last = V.tensor_scalar(xn[which][:, t, :], src[:, t, :], mv[which][:, t, 0:1], rstd[which][:, t:t + 1],
                                           ALU.subtract, ALU.mult)
                last.then_inc(xn_done[which], 1)

            def add_side(b):
                dve.wait_ge(sim_made, b.n + 1)
                dve.wait_ge(sided_b, b.n + 1)
                if b.at_least(2):
                    dve.wait_ge(pt_made, b.n - 1)
                V.scalar_tensor_tensor(out=att[b.c % 2][:, :, :], in0=sim_ps[:, 0:TT * J].rearrange("p (t j) -> p t j", t=TT), scalar=SC,
                                       in1=sided[b.c % 2][:, :, :], op0=ALU.mult, op1=ALU.add).then_inc(att_done, 1)
                dve.wait_ge(att_done, b.n + 1)
                if b.at_least(1):
                    dve.wait_ge(exped, b.n)
                V.tensor_reduce(negmax[:, :], att[b.c % 2][:, :, :], AX.X, ALU.max, negate=True).then_inc(max_done, 1)

            def invert(b):
                dve.wait_ge(exped, b.n + 1)
                V.reciprocal(rden[:, :], den[:, :]).then_inc(inverted, 1)

            def attended(b):
                dve.wait_ge(inverted, b.n + 1)
                dve.wait_ge(pv_made, b.n + 1)
                if b.at_least(4):
                    dve.wait_ge(res_done, b.n - 3)
                for t in range(TT):
                    last = V.scalar_tensor_tensor(out=x3[b.c % 4][:, t, :], in0=pv_ps[:, t * D:(t + 1) * D], scalar=rden[:, t:t + 1],
                                                  in1=x2[b.c % 4][:, t, :], op0=ALU.mult, op1=ALU.add)
                last.then_inc(x3_done, 1)
                dve.wait_ge(x3_done, b.n + 1)
                statistics(1, b, x3[b.c % 4])

            def biased(b):
                dve.wait_ge(ff_made, b.n + 1)
                if b.at_least(1):
                    dve.wait_ge(res_done, b.n)
                V.tensor_tensor(pre[:, :, :], ff_ps[:, :].rearrange("p (t c) -> p t c", t=TT),
                                bias_w[:, :].unsqueeze(1).to_broadcast([P, TT, D]), ALU.add).then_inc(pre_done, 1)

            def body(n):
                b1, b2, b3, b4, b5 = (n.shift(-lag) for lag in range(1, 6))
                if b3.real():
                    invert(b3)
                if b4.real():
                    normal(1, b4, x3[b4.c % 4])
                if b1.real():
                    normal(0, b1, x2[b1.c % 4])
                if b2.real():
                    add_side(b2)
                if b5.real():
                    biased(b5)
                if b3.real():
                    attended(b3)
                if n.real():
                    dve.wait_ge(x_in[n.c % 4], 16 * (n.turn(4) + 1))
                    statistics(0, n, x2[n.c % 4])

            loop(dve, body, LAGS)


def clear_semaphores(nc, sems):
    with nc.Block() as block:
        @block.gpsimd
        def _(pool):
            for s in sems:
                pool.sem_clear(s)


def make_identity(nc, ident):
    with nc.semaphore("identity_zero") as zeroed, nc.Block() as block:
        @block.gpsimd
        def _(pool):
            pool.memset(ident[:, :], 0.0).then_inc(zeroed, 1)
            pool.wait_ge(zeroed, 1)
            pool.affine_select(out=ident[:, :], in_=ident[:, :], compare_op=ALU.not_equal, fill=1.0, base=0,
                               pattern=[[-1, P]], channel_multiplier=1).then_inc(zeroed, 1)
            pool.wait_ge(zeroed, 2)


def rows_first(w):
    w = w.T
    return w.reshape(w.shape[0] // P, P, w.shape[1]).transpose(1, 0, 2)


def tiled(w):
    return w.reshape(w.shape[0] // P, P, w.shape[1]).transpose(1, 0, 2)


def layout(inputs):
    import numpy as np

    a = {k: np.asarray(v) for k, v in inputs.items()}
    wk, wv = a["L0_xattn_Wkv"][:INNER], a["L0_xattn_Wkv"][INNER:]
    ctx = a["ctx_1024"].transpose(0, 2, 1).reshape(B, KD, P, J).transpose(0, 2, 1, 3)
    return {
        "x": a["x"], "ctxt": ctx, "mask": a["mask_BxS2_bf1"].view(np.uint8),
        "wqt": rows_first(a["L0_xattn_Wq"]).reshape(P, -1), "wkt": rows_first(wk),
        "wvt": rows_first(wv).reshape(P, -1), "wot": rows_first(a["L0_xattn_Wout"]).reshape(P, -1),
        "bout": a["L0_xattn_b_out"], "wgt": rows_first(a["L0_ffn_Wg"]),
        "wq1": tiled(a["L1_xattn_Wq"]), "wk1": tiled(a["L1_xattn_Wk"]), "wv1t": rows_first(a["L1_xattn_Wv"]),
        "ffwt": rows_first(a["L1_ffn_weight"]), "ffa1": tiled(a["L1_ffn_aux_weight1"]), "ffa2": tiled(a["L1_ffn_aux_weight2"]),
        "we": np.stack([np.stack([rows_first(a[w][e]).reshape(P, -1) for w in ("L0_ffn_W1", "L0_ffn_W3", "L0_ffn_W2")], 1) for e in range(E)]),
        "wg": a["L0_ffn_Wg"], "fside": a["fside_BxSxS2_0"], "ffb": a["L1_ffn_bias"],
        "betas": np.stack([a["L1_xattn_beta_risk"], a["L1_xattn_beta_prio"], a["L1_xattn_beta_impl"]]),
        "bq": a["L1_xattn_bq"].reshape(KD, P).T, "bk": a["L1_xattn_bk"].reshape(KD, P).T, "bv": a["L1_xattn_bv"],
    }


def program(nc, io, out_dram):
    x1_dram = nc.dram_tensor("x1", [B * S, D], F32, kind="Internal").ap()
    xn1_dram = nc.dram_tensor("xn1", [B * S, D], F32, kind="Internal").ap()
    slots_dram = nc.dram_tensor("slot_tokens", [E, CAP], U32, kind="Internal").ap()
    with ExitStack() as ctx:
        def sb(name, shape, dt=F32):
            return ctx.enter_context(nc.sbuf_tensor(name, shape, dt))

        ident = sb("ident", [P, P])
        scores = sb("scores", [P, E, NT])
        make_identity(nc, ident)
        first_attention(nc, io, x1_dram, xn1_dram, ident, scores)
        expert_max, expert_inv = sb("expert_max", [P, E]), sb("expert_inv", [P, E])
        second = (sb("second_fold", [P, KD, D]), sb("second_keys", [P, B * KD, J]), sb("second_bias", [P, B, J]),
                  sb("second_values", [J, B, D]), sb("second_ffn", [P, KD, D]))
        route(nc, io, scores, slots_dram, expert_max, expert_inv, second)
        experts(nc, io, x1_dram, xn1_dram, slots_dram, ident, expert_max, expert_inv)
        second_layer(nc, io, x1_dram, out_dram, ident, second)


def kernel(**inputs):
    import numpy as np
    import concourse.bacc as bacc
    from concourse.bass_utils import run_bass_kernel_spmd

    nc = bacc.Bacc("TRN2", target_bir_lowering=False, num_devices=1)
    arrays, io = {}, {}
    for name, a in layout(inputs).items():
        a = np.ascontiguousarray(a)
        arrays[f"in_{name}"] = a
        io[name] = nc.dram_tensor(f"in_{name}", a.shape, mybir.dt.from_np(a.dtype), kind="ExternalInput").ap()
    out_dram = nc.dram_tensor("out", [B, S, D], F32, kind="ExternalOutput").ap()
    program(nc, io, out_dram)
    result = run_bass_kernel_spmd(nc, [arrays], core_ids=[0])
    return result.results[0]["out"]
```

```python
from contextlib import ExitStack

import concourse.bass as bass
from concourse import mybir

ALU = mybir.AluOpType
ACT = mybir.ActivationFunctionType
AX = mybir.AxisListType
F32 = mybir.dt.float32
F32R = mybir.dt.float32r
I32 = mybir.dt.int32
U32 = mybir.dt.uint32
U8 = mybir.dt.uint8
BF16 = mybir.dt.bfloat16

P = 128
B, S, D = 16, 256, 256
J = 120
H, DH = 16, 64
INNER = H * DH
TT = S // P
KD = D // P
MI = INNER // P
GROUPS = 4
HG = H // GROUPS
NT = B * TT
E, CAP, HID = 8, 512, 512
QT = CAP // P
HT = HID // P
EPS = 1e-5
NEG = -3.0e38

SECOND_SEMAPHORES = (
    "small_in x_in0 x_in1 x_in2 x_in3 side_in0 side_in1 pre_set coef_set sided_a sided_b bn0 bn1 mv0 mv1 "
    "var0 var1 half_set rstd0 rstd1 xn0 xn1 xt_made0 xt_made1 xt_out0 xt_out1 sim_made att_done max_done "
    "exped inverted pt_made pt_out pv_made x3_done ff_made pre_done tanh_done res_done stored0 stored1"
).split()


class Batch:

    def __init__(self, i, c):
        self.i, self.c, self.par = i, c, c % 2
        self.turn = i + c // 2
        self.n = 2 * i + c

    def shift(self, d):
        return Batch(self.i, self.c + d)

    def real(self):
        return not isinstance(self.n, int) or 0 <= self.n < B

    def at_least(self, n):
        return not isinstance(self.n, int) or self.n >= n


class Batch4:

    def __init__(self, i, c):
        self.i, self.c, self.n = i, c, 4 * i + c

    def turn(self, ring):
        return (4 // ring) * self.i + self.c // ring

    def shift(self, d):
        return Batch4(self.i, self.c + d)

    def real(self):
        return not isinstance(self.n, int) or 0 <= self.n < B

    def at_least(self, n):
        return not isinstance(self.n, int) or self.n >= n


def pipeline(eng, body):
    for n in range(-1, 4):
        body(Batch(0, n))
    with eng.Fori(2, (B - 2) // 2) as i:
        for c in range(2):
            body(Batch(i, c))
    for n in range(B - 2, B + 2):
        body(Batch(0, n))


def first_attention(nc, io, x1_dram, xn1_dram, ident, scores):
    with ExitStack() as ctx:
        def sb(name, shape, dt=F32):
            return ctx.enter_context(nc.sbuf_tensor("a_" + name, shape, dt))

        def ps(name):
            return ctx.enter_context(nc.psum_tensor("ap_" + name, [P, 512], F32))

        def sem(name):
            return ctx.enter_context(nc.semaphore("a_" + name))

        wq = [sb(f"wq{s}", [P, KD, INNER], F32R) for s in ("hi", "lo")]
        wv = [sb(f"wv{s}", [P, KD, INNER], F32R) for s in ("hi", "lo")]
        wo = [sb(f"wo{s}", [P, MI, D], F32R) for s in ("hi", "lo")]
        wk = sb("wk", [P, KD, INNER])
        stage = [sb(f"stage{n}", [P, KD * INNER]) for n in range(2)]
        wgt = sb("wgt", [P, KD, E])
        bout = sb("bout", [P, D])
        neghalf = sb("neghalf", [P, TT])
        turnstile = sb("turnstile", [P, 1])
        xin = [sb(f"xin{n}", [P, TT, D]) for n in range(2)]
        xres = [sb(f"xres{n}", [P, TT, D]) for n in range(2)]
        ctxt = [sb(f"ctxt{n}", [P, KD, J]) for n in range(2)]
        ctxh = [sb(f"ctxh{n}", [P, KD, J], F32R) for n in range(2)]
        ctxl = [sb(f"ctxl{n}", [P, KD, J], F32R) for n in range(2)]
        mask8 = sb("mask8", [P, B * J], U8)
        bias = sb("bias", [P, B, J], BF16)
        xn = sb("xn", [P, TT, D])
        xnh = sb("xnh", [P, KD, S], F32R)
        xnl = sb("xnl", [P, KD, S], F32R)
        qt = [sb(f"qt{n}", [P, MI, S]) for n in range(2)]
        kt = [sb(f"kt{n}", [P, MI, J]) for n in range(2)]
        vh = [sb(f"vh{n}", [J, INNER], F32R) for n in range(2)]
        vl = [sb(f"vl{n}", [J, INNER], F32R) for n in range(2)]
        prob = [sb(f"prob{n}", [P, 2, TT * 2, J]) for n in range(4)]
        negmax = [sb(f"negmax{n}", [P, 2, TT * 2]) for n in range(2)]
        den = [sb(f"den{n}", [P, 2, TT * 2]) for n in range(2)]
        rden = [sb(f"rden{n}", [P, 2, TT * 2]) for n in range(2)]
        pth = [sb(f"pth{n}", [J, 2, 2, S], F32R) for n in range(2)]
        ptl = [sb(f"ptl{n}", [J, 2, 2, S], F32R) for n in range(2)]
        oth = sb("oth", [P, MI, S], F32R)
        otl = sb("otl", [P, MI, S], F32R)
        x1 = [sb(f"x1{n}", [P, TT, D]) for n in range(2)]
        xn1 = [sb(f"xn1{n}", [P, TT, D]) for n in range(2)]
        x1t = sb("x1t", [P, KD, S])
        bn = [sb(f"bn{n}", [P, TT, 6]) for n in range(2)]
        mv = [sb(f"mv{n}", [P, TT, 2]) for n in range(2)]
        var = [sb(f"var{n}", [P, TT]) for n in range(2)]
        rstd = [sb(f"rstd{n}", [P, TT]) for n in range(2)]

        sim_ps = [ps("sim0"), ps("sim1")]
        t_ps = [ps("t0"), ps("t1")]
        pv_ps = [ps("pv0"), ps("pv1")]
        job_ps = [ps("job0"), ps("job1")]

        w_in = [sem(f"w_in{n}") for n in range(2)]
        wk_in, small_in = sem("wk_in"), sem("small_in")
        w_hi, w_lo = sem("w_hi"), sem("w_lo")
        x_in = [sem(f"x_in{n}") for n in range(2)]
        xres_in = [sem(f"xres_in{n}") for n in range(2)]
        ctx_in = [sem(f"ctx_in{n}") for n in range(2)]
        mask_in = sem("mask_in")
        half_set = sem("half_set")
        ctx_hi, ctx_lo, bias_set = sem("ctx_hi"), sem("ctx_lo"), sem("bias_set")
        bn_done = [sem("bn_x"), sem("bn_x1")]
        mv_done = [sem("mv_x"), sem("mv_x1")]
        var_done = [sem("var_x"), sem("var_x1")]
        rstd_done = [sem("rstd_x"), sem("rstd_x1")]
        xn_done, x1_done, xn1_done = sem("xn_done"), sem("x1_done"), sem("xn1_done")
        kinds = ("xt", "v", "k", "q", "y", "x1t", "gate")
        made = {k: sem("made_" + k) for k in kinds}
        out = {k: sem("out_" + k) for k in kinds}
        xt_hi, v_hi = sem("xt_hi"), sem("v_hi")
        sim_done, biased, maxed, shifted = sem("sim_done"), sem("biased"), sem("maxed"), sem("shifted")
        exped, summed, inverted, normed = sem("exped"), sem("summed"), sem("inverted"), sem("normed")
        pt_made, pt_hi, pt_lo = sem("pt_made"), sem("pt_hi"), sem("pt_lo")
        pv_done, o_hi, o_lo = sem("pv_done"), sem("o_hi"), sem("o_lo")
        x1_stored = [sem(f"x1_stored{n}") for n in range(2)]
        xn1_stored = [sem(f"xn1_stored{n}") for n in range(2)]

        x_dram = io["x"].rearrange("b (t p) c -> b p t c", p=P)
        x1_out = x1_dram.rearrange("(b t p) c -> b p t c", p=P, t=TT)
        xn1_out = xn1_dram.rearrange("(b t p) c -> b p t c", p=P, t=TT)

        JOBS = [[("xt", 1, 0), ("k", 1, 0), ("k", 1, 1)],
                [("q", 1, 0), ("q", 1, 1), ("x1t", -2, 0)],
                [("q", 1, 2), ("y", -1, 0), ("v", 1, 0)],
                [("q", 1, 3), ("v", 1, 1), ("gate", -2, 0)]]
        PARTS = {"xt": 1, "v": 2, "k": 2, "q": 4, "y": 1, "x1t": 1, "gate": 1}
        flat = [job for step in JOBS for job in step]

        def job_bank(g, n):
            return job_ps[(3 * g + n) % 2]

        def before_last(beta, g, n):
            for at in range(3 * g + n - 2, -2 * len(flat), -2):
                kind, rel, part = flat[at % len(flat)]
                b = beta.shift(rel + at // len(flat))
                if b.real():
                    return kind, b, part
            return None

        def count(kind, b, part):
            return PARTS[kind] * b.n + part + 1

        def groups(beta, g):
            late = (beta.shift(-1), g + 2) if g < 2 else (beta, g - 2)
            return (beta, g), late

        def nth(b, g):
            return GROUPS * b.n + g

        block = ctx.enter_context(nc.Block())

        @block.sync
        def _(sp):
            def loads(b):
                p = b.par
                if b.at_least(2):
                    sp.wait_ge(xn_done, b.n - 1)
                sp.dma_start(xin[p][:, :, :], x_dram[b.n]).then_inc(x_in[p], 16)
                if b.at_least(2):
                    sp.wait_ge(made["k"], 2 * (b.n - 1))
                    sp.wait_ge(ctx_lo, b.n - 1)
                sp.dma_start(ctxt[p][:, :, :], io["ctxt"][b.n]).then_inc(ctx_in[p], 16)

            def load_residual(b):
                if b.at_least(2):
                    sp.wait_ge(x1_done, b.n - 1)
                sp.dma_start(xres[b.par][:, :, :], x_dram[b.n]).then_inc(xres_in[b.par], 16)

            loads(Batch(0, 0))
            sp.dma_start(wk[:, :, :], io["wkt"]).then_inc(wk_in, 16)
            sp.dma_start(stage[0][:, :], io["wqt"]).then_inc(w_in[0], 16)
            loads(Batch(0, 1))
            sp.dma_start(stage[1][:, :], io["wvt"]).then_inc(w_in[1], 16)
            sp.dma_start(bout[:, :], io["bout"].rearrange("(a c) -> a c", a=1).to_broadcast([P, D])).then_inc(small_in, 16)
            sp.dma_start(wgt[:, :, :], io["wgt"]).then_inc(small_in, 16)
            sp.dma_start(mask8[:, :], io["mask"].rearrange("(a b) j -> a (b j)", a=1).to_broadcast([P, B * J])).then_inc(mask_in, 16)
            sp.wait_ge(w_lo, 1)
            sp.dma_start(stage[0][:, :], io["wot"]).then_inc(w_in[0], 16)

            def block_of(beta):
                if beta.shift(2).real() and beta.shift(2).at_least(2):
                    loads(beta.shift(2))
                b = beta.shift(-2)
                if b.real():
                    sp.wait_ge(x1_done, b.n + 1)
                    sp.dma_start(x1_out[b.n], x1[b.par][:, :, :]).then_inc(x1_stored[b.par], 16)
                    sp.wait_ge(xn1_done, b.n + 1)
                    sp.dma_start(xn1_out[b.n], xn1[b.par][:, :, :]).then_inc(xn1_stored[b.par], 16)
                if beta.shift(1).real():
                    load_residual(beta.shift(1))

            pipeline(sp, block_of)
            for n in range(2):
                sp.wait_ge(x1_stored[n], 16 * (B // 2))
                sp.wait_ge(xn1_stored[n], 16 * (B // 2))

        @block.tensor
        def _(pe):
            def mm3(out_ap, lhs, rhs, start, stop):
                (lh, ll), (rh, rl) = lhs, rhs
                nc.tensor.matmul(out_ap, lh, rh, start=start, stop=False)
                nc.tensor.matmul(out_ap, lh, rl, start=False, stop=False)
                return nc.tensor.matmul(out_ap, ll, rh, start=False, stop=stop)

            def job(beta, g, n):
                kind, rel, part = JOBS[g][n]
                b = beta.shift(rel)
                if not b.real():
                    return
                before = before_last(beta, g, n)
                if before:
                    pe.wait_ge(out[before[0]], count(*before))
                bank, p = job_bank(g, n), b.par
                if kind == "xt":
                    pe.wait_ge(xn_done, b.n + 1)
                    for t in range(TT):
                        for k in range(KD):
                            last = nc.tensor.transpose(bank[:, k * S + t * P:k * S + (t + 1) * P],
                                                       xn[:, t, k * P:(k + 1) * P], ident[:, :])
                elif kind == "v":
                    if part == 0:
                        pe.wait_ge(ctx_hi, b.n + 1)
                        pe.wait_ge(ctx_lo, b.n + 1)
                        if not b.at_least(1):
                            pe.wait_ge(w_hi, 2)
                            pe.wait_ge(w_lo, 2)
                    for k in range(KD):
                        cols = slice(part * 512, part * 512 + 512)
                        last = mm3(bank[0:J, :], (ctxh[p][:, k, :], ctxl[p][:, k, :]),
                                   (wv[0][:, k, cols], wv[1][:, k, cols]), k == 0, k == KD - 1)
                elif kind == "k":
                    if part == 0:
                        pe.wait_ge(ctx_in[p], 16 * (b.turn + 1))
                        if not b.at_least(1):
                            pe.wait_ge(wk_in, 16)
                    for m in range(4):
                        for k in range(KD):
                            mi = 4 * part + m
                            last = nc.tensor.matmul(bank[:, m * J:(m + 1) * J], wk[:, k, mi * P:(mi + 1) * P],
                                                    ctxt[p][:, k, :], start=k == 0, stop=k == KD - 1)
                elif kind == "q":
                    if part == 0:
                        pe.wait_ge(xt_hi, b.n + 1)
                        pe.wait_ge(out["xt"], b.n + 1)
                        if not b.at_least(1):
                            pe.wait_ge(w_hi, 1)
                            pe.wait_ge(w_lo, 1)
                    for m in range(2):
                        mi = 2 * part + m
                        cols = slice(mi * P, mi * P + P)
                        for k in range(KD):
                            last = mm3(bank[:, m * S:(m + 1) * S], (wq[0][:, k, cols], wq[1][:, k, cols]),
                                       (xnh[:, k, :], xnl[:, k, :]), k == 0, k == KD - 1)
                elif kind == "y":
                    pe.wait_ge(o_hi, 2 * nth(b, GROUPS))
                    pe.wait_ge(o_lo, 2 * nth(b, GROUPS))
                    if not b.at_least(1):
                        pe.wait_ge(w_hi, 3)
                        pe.wait_ge(w_lo, 3)
                    for t in range(TT):
                        rows = slice(t * P, (t + 1) * P)
                        for m in range(MI):
                            last = mm3(bank[:, t * D:(t + 1) * D], (oth[:, m, rows], otl[:, m, rows]),
                                       (wo[0][:, m, :], wo[1][:, m, :]), m == 0, m == MI - 1)
                elif kind == "x1t":
                    pe.wait_ge(xn1_done, b.n + 1)
                    for t in range(TT):
                        for k in range(KD):
                            last = nc.tensor.transpose(bank[:, k * S + t * P:k * S + (t + 1) * P],
                                                       xn1[p][:, t, k * P:(k + 1) * P], ident[:, :])
                else:
                    pe.wait_ge(out["x1t"], b.n + 1)
                    for t in range(TT):
                        for k in range(KD):
                            last = nc.tensor.matmul(bank[:, t * E:(t + 1) * E], x1t[:, k, t * P:(t + 1) * P],
                                                    wgt[:, k, :], start=k == 0, stop=k == KD - 1)
                last.then_inc(made[kind], 1)

            def sim(b, g):
                pe.wait_ge(out["k"], 2 * b.n + g // 2 + 1)
                pe.wait_ge(out["q"], 4 * b.n + g + 1)
                n = nth(b, g)
                if g or b.at_least(1):
                    pe.wait_ge(biased, 2 * n)
                for t in range(TT):
                    for hh in range(2):
                        for odd in range(2):
                            m, rows = 2 * g + hh, slice(DH * odd, DH * odd + DH)
                            at = (t * 2 + hh) * J
                            last = nc.tensor.matmul(sim_ps[odd][:, at:at + J], qt[b.par][rows, m, t * P:(t + 1) * P],
                                                    kt[b.par][rows, m, :], start=True, stop=True)
                            if t == TT - 1 and hh == 1:
                                last.then_inc(sim_done, 1)

            def transposes(b, g):
                n = nth(b, g)
                for odd in range(2):
                    pe.wait_ge(normed, 2 * n + odd + 1)
                    if g or b.at_least(1):
                        pe.wait_ge(pt_lo, 2 * n - 2 + odd + 1)
                    for hh in range(2):
                        for t in range(TT):
                            last = nc.tensor.transpose(t_ps[odd][0:J, hh * S + t * P:hh * S + (t + 1) * P],
                                                       prob[g % 4][:, odd, t * 2 + hh, :], ident[:, :])
                    last.then_inc(pt_made, 1)

            def values(b, g):
                n = nth(b, g)
                if g == 0:
                    pe.wait_ge(v_hi, 2 * b.n + 2)
                    pe.wait_ge(out["v"], 2 * b.n + 2)
                for odd in range(2):
                    pe.wait_ge(pt_hi, 2 * n + odd + 1)
                    pe.wait_ge(pt_lo, 2 * n + odd + 1)
                    if g or b.at_least(1):
                        pe.wait_ge(o_lo, 2 * n - 2 + odd + 1)
                    for hh in range(2):
                        h = HG * g + 2 * hh + odd
                        cols = slice(h * DH, h * DH + DH)
                        last = mm3(pv_ps[odd][0:DH, hh * S:(hh + 1) * S], (vh[b.par][:, cols], vl[b.par][:, cols]),
                                   (pth[g % 2][:, odd, hh, :], ptl[g % 2][:, odd, hh, :]), True, True)
                    last.then_inc(pv_done, 1)

            def block_of(beta):
                for g in range(GROUPS):
                    (b, g1), (b2, g2) = groups(beta, g)
                    if b.real():
                        sim(b, g1)
                    if b2.real():
                        transposes(b2, g2)
                    for n in range(3):
                        job(beta, g, n)
                    if b2.real():
                        values(b2, g2)

            pipeline(pe, block_of)

        @block.scalar
        def _(act):
            def staged_leading(n):
                w, half = ((wq, 0), (wv, 1), (wo, 0))[n]
                act.wait_ge(w_in[half], 16 * (n // 2 + 1))
                nc.scalar.copy(w[0][:, :, :].rearrange("p a b -> p (a b)"), stage[half][:, :]).then_inc(w_hi, 1)

            act.wait_ge(ctx_in[0], 16)
            nc.scalar.copy(ctxh[0][:, :, :], ctxt[0][:, :, :]).then_inc(ctx_hi, 1)

            def job(beta, g, n):
                kind, rel, part = JOBS[g][n]
                b = beta.shift(rel)
                if not b.real() or kind in ("y", "gate"):
                    return
                bank, p = job_bank(g, n), b.par
                act.wait_ge(made[kind], count(kind, b, part))
                if kind == "xt":
                    if b.at_least(1):
                        act.wait_ge(made["q"], 4 * b.n)
                    nc.scalar.copy(xnh[:, :, :].rearrange("p a b -> p (a b)"), bank[:, :]).then_inc(xt_hi, 1)
                elif kind == "v":
                    if part == 0 and b.at_least(2):
                        act.wait_ge(pv_done, 2 * nth(b.shift(-2), GROUPS))
                    nc.scalar.copy(vh[p][:, part * 512:part * 512 + 512], bank[0:J, :]).then_inc(v_hi, 1)
                elif kind == "k":
                    if part == 0 and b.at_least(2):
                        act.wait_ge(sim_done, 2 * nth(b.shift(-2), GROUPS))
                    nc.scalar.copy(kt[p][:, 4 * part:4 * part + 4, :].rearrange("p a b -> p (a b)"),
                                   bank[:, 0:4 * J]).then_inc(out["k"], 1)
                elif kind == "q":
                    if part == 0 and b.at_least(2):
                        act.wait_ge(sim_done, 2 * nth(b.shift(-2), GROUPS))
                    nc.scalar.copy(qt[p][:, 2 * part:2 * part + 2, :].rearrange("p a b -> p (a b)"),
                                   bank[:, :]).then_inc(out["q"], 1)
                elif kind == "x1t":
                    if b.at_least(1):
                        act.wait_ge(made["gate"], b.n)
                    nc.scalar.copy(x1t[:, :, :].rearrange("p a b -> p (a b)"), bank[:, :]).then_inc(out["x1t"], 1)

            def pt_leading(b, g):
                n = nth(b, g)
                for odd in range(2):
                    act.wait_ge(pt_made, 2 * n + odd + 1)
                    if b.at_least(1) or g >= 2:
                        act.wait_ge(pv_done, 2 * (n - 2) + odd + 1)
                    nc.scalar.copy(pth[g % 2][:, odd, :, :].rearrange("p a b -> p (a b)"),
                                   t_ps[odd][0:J, :]).then_inc(pt_hi, 1)

            def out_leading(b, g):
                n = nth(b, g)
                if g == 0 and b.at_least(1):
                    act.wait_ge(made["y"], b.n)
                for odd in range(2):
                    act.wait_ge(pv_done, 2 * n + odd + 1)
                    nc.scalar.copy(oth[DH * odd:DH * odd + DH, 2 * g:2 * g + 2, :].rearrange("p a b -> p (a b)"),
                                   pv_ps[odd][0:DH, :]).then_inc(o_hi, 1)

            def exps(b, g):
                n = nth(b, g)
                for odd in range(2):
                    act.wait_ge(shifted, 2 * n + odd + 1)
                    ap = prob[g % 4][:, odd, :, :]
                    nc.scalar.activation(ap, ap, ACT.Exp, scale=DH ** -0.5).then_inc(exped, 1)

            def block_of(beta):
                for g in range(GROUPS):
                    (b, g1), (b2, g2) = groups(beta, g)
                    if b2.real():
                        pt_leading(b2, g2)
                    for n in range(2):
                        job(beta, g, n)
                    if not beta.at_least(0) and g == 0:
                        staged_leading(0)
                    if b.real():
                        exps(b, g1)
                    job(beta, g, 2)
                    if b2.real():
                        out_leading(b2, g2)
                    if not beta.at_least(0) and g < 2:
                        staged_leading(g + 1)
                        if g == 0:
                            act.wait_ge(ctx_in[1], 16)
                            nc.scalar.copy(ctxh[1][:, :, :], ctxt[1][:, :, :]).then_inc(ctx_hi, 1)
                    if g == 1 and beta.shift(2).real() and beta.shift(2).at_least(2):
                        c = beta.shift(2)
                        act.wait_ge(ctx_in[c.par], 16 * (c.turn + 1))
                        act.wait_ge(made["v"], 2 * (c.n - 1))
                        nc.scalar.copy(ctxh[c.par][:, :, :], ctxt[c.par][:, :, :]).then_inc(ctx_hi, 1)

            pipeline(act, block_of)

        @block.gpsimd
        def _(pool):
            pool.memset(neghalf[:, :], -0.5).then_inc(half_set, 1)
            pool.wait_ge(half_set, 1)

            def rsqrt(which, b):
                pool.wait_ge(var_done[which], b.n + 1)
                nc.gpsimd.tensor_tensor(rstd[which][:, :], var[which][:, :], neghalf[:, :],
                                        ALU.pow).then_inc(rstd_done[which], 1)

            def shift(b, g):
                n = nth(b, g)
                for odd in range(2):
                    pool.wait_ge(maxed, 2 * n + odd + 1)
                    ap = prob[g % 4][:, odd, :, :]
                    nc.gpsimd.tensor_tensor(ap, ap, negmax[g % 2][:, odd, :].unsqueeze(2).to_broadcast([P, TT * 2, J]),
                                            ALU.add).then_inc(shifted, 1)

            def normalise(b, g):
                n = nth(b, g)
                pool.wait_ge(inverted, n + 1)
                for odd in range(2):
                    ap = prob[g % 4][:, odd, :, :]
                    nc.gpsimd.tensor_tensor(ap, ap, rden[g % 2][:, odd, :].unsqueeze(2).to_broadcast([P, TT * 2, J]),
                                            ALU.mult).then_inc(normed, 1)

            rsqrt(0, Batch(0, 0))

            def block_of(beta):
                for g in range(GROUPS):
                    (b, g1), _ = groups(beta, g)
                    if b.real():
                        shift(b, g1)
                    if g == 0 and beta.shift(-1).real():
                        normalise(beta.shift(-1), GROUPS - 1)
                    if g and b.real():
                        normalise(b, g - 1)
                    if g == 2 and beta.shift(2).real() and beta.shift(2).at_least(1):
                        rsqrt(0, beta.shift(2))
                    if g == 2 and beta.shift(-1).real():
                        rsqrt(1, beta.shift(-1))

            pipeline(pool, block_of)

        @block.vector
        def _(dve):
            def lower(out_ap, whole, hi, signal):
                return nc.vector.tensor_tensor(out_ap, whole, hi.bitcast(F32), ALU.subtract).then_inc(signal, 1)

            def statistics(which, b, src):
                for t in range(TT):
                    last = nc.vector.bn_stats(bn[which][:, t, :], src[:, t, :])
                last.then_inc(bn_done[which], 1)
                dve.wait_ge(bn_done[which], b.n + 1)
                nc.vector.memset(turnstile[:, :], 0.0)
                for t in range(TT):
                    last = nc.vector.bn_aggr(mv[which][:, t, :], bn[which][:, t, :])
                last.then_inc(mv_done[which], 1)
                dve.wait_ge(mv_done[which], b.n + 1)
                nc.vector.tensor_scalar(var[which][:, :], mv[which][:, :, 1], EPS, None, ALU.add).then_inc(var_done[which], 1)

            def normal(which, b, src, dst, signal):
                dve.wait_ge(rstd_done[which], b.n + 1)
                for t in range(TT):
                    last = nc.vector.tensor_scalar(dst[:, t, :], src[:, t, :], mv[which][:, t, 0:1], rstd[which][:, t:t + 1],
                                                   ALU.subtract, ALU.mult)
                last.then_inc(signal, 1)

            def normal_x(b):
                if b.at_least(1):
                    dve.wait_ge(made["xt"], b.n)
                normal(0, b, xin[b.par], xn, xn_done)

            def split_context(b):
                dve.wait_ge(ctx_hi, b.n + 1)
                lower(ctxl[b.par][:, :, :], ctxt[b.par][:, :, :], ctxh[b.par][:, :, :], ctx_lo)

            def staged_rest(n):
                w, half = ((wq, 0), (wv, 1), (wo, 0))[n]
                dve.wait_ge(w_hi, n + 1)
                lower(w[1][:, :, :].rearrange("p a b -> p (a b)"), stage[half][:, :],
                      w[0][:, :, :].rearrange("p a b -> p (a b)"), w_lo)

            dve.wait_ge(x_in[0], 16)
            statistics(0, Batch(0, 0), xin[0])
            split_context(Batch(0, 0))
            normal_x(Batch(0, 0))

            def job(beta, g, n):
                kind, rel, part = JOBS[g][n]
                b = beta.shift(rel)
                if not b.real() or kind not in ("xt", "v", "y", "gate"):
                    return
                bank, p = job_bank(g, n), b.par
                if kind == "xt":
                    dve.wait_ge(xt_hi, b.n + 1)
                    lower(xnl[:, :, :].rearrange("p a b -> p (a b)"), bank[:, :],
                          xnh[:, :, :].rearrange("p a b -> p (a b)"), out["xt"])
                elif kind == "v":
                    dve.wait_ge(v_hi, 2 * b.n + part + 1)
                    cols = slice(part * 512, part * 512 + 512)
                    lower(vl[p][:, cols], bank[0:J, :], vh[p][:, cols], out["v"])
                elif kind == "y":
                    dve.wait_ge(made["y"], b.n + 1)
                    dve.wait_ge(xres_in[p], 16 * (b.turn + 1))
                    if b.at_least(2):
                        dve.wait_ge(x1_stored[p], 16 * b.turn)
                    nc.vector.tensor_tensor(x1[p][:, :, :], bank[:, :].rearrange("p (t c) -> p t c", t=TT),
                                            xres[p][:, :, :], ALU.add).then_inc(out["y"], 1)
                    dve.wait_ge(out["y"], b.n + 1)
                    nc.vector.tensor_tensor(x1[p][:, :, :], x1[p][:, :, :],
                                            bout[:, :].unsqueeze(1).to_broadcast([P, TT, D]), ALU.add).then_inc(x1_done, 1)
                    dve.wait_ge(x1_done, b.n + 1)
                    statistics(1, b, x1[p])
                else:
                    dve.wait_ge(made["gate"], b.n + 1)
                    nc.vector.tensor_copy(scores[:, :, bass.ds(TT * b.n, TT)].rearrange("p e t -> p t e"),
                                          bank[:, 0:TT * E].rearrange("p (t e) -> p t e", t=TT)).then_inc(out["gate"], 1)

            def add_bias(b, g):
                n = nth(b, g)
                if g == 0 and not b.at_least(1):
                    dve.wait_ge(bias_set, 1)
                for odd in range(2):
                    dve.wait_ge(sim_done, 2 * n + odd + 1)
                    if b.at_least(1):
                        dve.wait_ge(pt_made, 2 * (n - 4) + odd + 1)
                    nc.vector.tensor_tensor(prob[g % 4][:, odd, :, :], sim_ps[odd][:, 0:4 * J].rearrange("p (a j) -> p a j", j=J),
                                            bias[:, bass.ds(b.n, 1), :].to_broadcast([P, 4, J]), ALU.add).then_inc(biased, 1)

            def maxima(b, g):
                n = nth(b, g)
                for odd in range(2):
                    dve.wait_ge(biased, 2 * n + odd + 1)
                    if b.at_least(1) or g >= 2:
                        dve.wait_ge(shifted, 2 * (n - 2) + odd + 1)
                    nc.vector.tensor_reduce(negmax[g % 2][:, odd, :], prob[g % 4][:, odd, :, :], AX.X, ALU.max,
                                            negate=True).then_inc(maxed, 1)

            def sums(b, g):
                n = nth(b, g)
                dve.wait_ge(exped, 2 * n + 2)
                if b.at_least(1) or g >= 1:
                    dve.wait_ge(normed, 2 * n)
                nc.vector.tensor_reduce(den[g % 2][:, :, :], prob[g % 4][:, :, :, :], AX.X, ALU.add).then_inc(summed, 1)
                dve.wait_ge(summed, n + 1)
                nc.vector.reciprocal(rden[g % 2][:, :, :], den[g % 2][:, :, :]).then_inc(inverted, 1)

            def pt_rest(b, g):
                n = nth(b, g)
                for odd in range(2):
                    dve.wait_ge(pt_hi, 2 * n + odd + 1)
                    lower(ptl[g % 2][:, odd, :, :].rearrange("p a b -> p (a b)"), t_ps[odd][0:J, :],
                          pth[g % 2][:, odd, :, :].rearrange("p a b -> p (a b)"), pt_lo)

            def out_rest(b, g):
                n = nth(b, g)
                for odd in range(2):
                    dve.wait_ge(o_hi, 2 * n + odd + 1)
                    rows = slice(DH * odd, DH * odd + DH)
                    lower(otl[rows, 2 * g:2 * g + 2, :].rearrange("p a b -> p (a b)"), pv_ps[odd][0:DH, :],
                          oth[rows, 2 * g:2 * g + 2, :].rearrange("p a b -> p (a b)"), o_lo)

            def block_of(beta):
                for g in range(GROUPS):
                    (b, g1), (b2, g2) = groups(beta, g)
                    if b.real():
                        add_bias(b, g1)
                    if g == 0:
                        job(beta, g, 0)
                    if b2.real():
                        pt_rest(b2, g2)
                    if b.real():
                        maxima(b, g1)
                    before = (b.shift(-1), GROUPS - 1) if g == 0 else (b, g - 1)
                    if before[0].real():
                        sums(*before)
                    if g == 3 and beta.shift(2).real() and beta.shift(2).at_least(1):
                        normal_x(beta.shift(2))
                    for n in range(g == 0, 2):
                        job(beta, g, n)
                    if not beta.at_least(0) and g == 0:
                        staged_rest(0)
                    job(beta, g, 2)
                    if b2.real():
                        out_rest(b2, g2)
                    if not beta.at_least(0) and g < 2:
                        staged_rest(g + 1)
                        if g == 0:
                            split_context(Batch(0, 1))
                            dve.wait_ge(mask_in, 16)
                            nc.vector.tensor_scalar(bias[:, :, :].rearrange("p b j -> p (b j)"), mask8[:, :], -NEG, NEG,
                                                    ALU.mult, ALU.add).then_inc(bias_set, 1)
                            dve.wait_ge(small_in, 32)
                    c, d = beta.shift(2), beta.shift(-1)
                    if g == 1 and c.real() and c.at_least(1):
                        dve.wait_ge(x_in[c.par], 16 * (c.turn + 1))
                        statistics(0, c, xin[c.par])
                        if c.at_least(2):
                            split_context(c)
                    if g == 3 and d.real():
                        if d.at_least(2):
                            dve.wait_ge(xn1_stored[d.par], 16 * d.turn)
                            dve.wait_ge(made["x1t"], d.n - 1)
                        normal(1, d, x1[d.par], xn1[d.par], xn1_done)

            pipeline(dve, block_of)


def route(nc, io, ident, scores, slots_dram, expert_max, expert_inv, second, weights, xn1_dram, slots, xg):
    gt, keys_m, keys_bias, values, ffn_w = second
    wraw, up_h, up_l, _, _ = weights
    with ExitStack() as ctx:
        def sb(name, shape, dt=F32):
            return ctx.enter_context(nc.sbuf_tensor("r_" + name, shape, dt))

        def ps(name):
            return ctx.enter_context(nc.psum_tensor("rp_" + name, [P, 512], F32))

        def sem(name):
            return ctx.enter_context(nc.semaphore("r_" + name))

        wide = [P, E, NT]
        ones = sb("ones", [P, P], BF16)
        tri = sb("tri", [P, P], BF16)
        blocks = sb("blocks", [P, P], BF16)
        keep = sb("keep", [P, E, NT])
        iota = sb("iota", [P, 32], I32)
        row = sb("row", [P, 1], I32)
        values_of = sb("values_of", [P, 32, NT], BF16)
        tile_no = sb("tile_no", [P, NT], BF16)
        row_no = sb("row_no", [P, 1])
        turned = sb("turned", [P, 2, P])
        reached = sb("reached", [P, 2, P], BF16)
        count2 = sb("count2", [P, 2], BF16)
        bits = [sb(f"bits{n}", [P, 2], U32) for n in range(2)]
        cand, flipped, back = (sb(n, [P, 2], U32) for n in ("cand", "flipped", "back"))
        limits = sb("limits", [P, 2, P], U32)
        count = sb("count", [P, E])
        over = sb("over", wide, BF16)
        equal = sb("equal", wide, BF16)
        need = sb("need", [P, E])
        total = sb("total", wide)
        whole = sb("whole", wide, I32)
        rank = sb("rank", wide)
        chosen = sb("chosen", wide, BF16)
        place = sb("place", wide)
        pmax = sb("pmax", [P, E])
        grown = sb("grown", wide)
        gsum = sb("gsum", [P, E])
        onesf = sb("onesf", [P, P])
        place_hi, place_lo = sb("place_hi", wide), sb("place_lo", wide)
        high, low = sb("high", wide, BF16), sb("low", wide, BF16)
        A = [sb(f"A{n}", [P, 32, NT], BF16) for n in range(2)]
        C = [sb(f"C{n}", [P, 2, 16, NT], BF16) for n in range(2)]
        slot = sb("slot", [32, E, 16], U32)
        slotf = sb("slotf", [32, E, 2, 16])

        wq_n, wk_n = sb("wq_n", [P, KD, D]), sb("wk_n", [P, KD, D])
        wv_t = sb("wv_t", [P, KD, D])
        w_t, a1_n, a2_n = sb("w_t", [P, KD, D]), sb("a1_n", [P, KD, D]), sb("a2_n", [P, KD, D])
        wa_t = sb("wa_t", [P, KD, D])
        bq, bk = sb("bq", [P, KD]), sb("bk", [P, KD])
        bv = sb("bv", [1, D])
        bqb = sb("bqb", [P, KD, P])
        w2b = sb("w2b", [P, KD, P])
        u = sb("u", [P, KD])
        s0 = sb("s0", [P, 1])
        ctxt = [sb(f"ctxt{n}", [P, KD, J]) for n in range(2)]

        cnt_ps = [ps("cnt0"), ps("cnt1")]
        sum_ps = ps("sum")
        fold_ps = ps("fold")
        m_ps = [ps("m0"), ps("m1")]
        v_ps = [ps("v0"), ps("v1")]
        square_ps, column_ps = (fold_ps, m_ps[1], v_ps[1]), v_ps[0]

        fold_in = [sem("fold_in0"), sem("fold_in1")]
        w_in, expert_in, expert_hi, expert_lo = sem("w_in"), sem("expert_in"), sem("expert_hi"), sem("expert_lo")
        consts, ones_set, zero_tri, tri_set, iota_set = sem("consts"), sem("ones_set"), sem("zero_tri"), sem("tri_set"), sem("iota_set")
        blocks_zero, blocks_set, turn_made, turn_read = sem("blocks_zero"), sem("blocks_set"), sem("turn_made"), sem("turn_read")
        bit_set, cand_set, flip_set, back_set = sem("bit_set"), sem("cand_set"), sem("flip_set"), sem("back_set")
        over_set, counted, limits_set = sem("over_set"), sem("counted"), sem("limits_set")
        step_done, ranked = sem("step_done"), sem("ranked")
        max_set, max_all, grown_set = sem("max_set"), sem("max_all"), sem("grown_set")
        onehot, gathered, slot_set = sem("onehot"), sem("gathered"), sem("slot_set")
        slots_stored, first_slot, first_in, first_gathered = (sem(n) for n in ("slots_stored", "first_slot", "first_in", "first_gathered"))
        ctx_in = [sem(f"ctx_in{n}") for n in range(2)]
        folded, fold_read, bc_set = sem("folded"), sem("fold_read"), sem("bc_set")
        m_made, m_read, v_made, v_read = sem("m_made"), sem("m_read"), sem("v_made"), sem("v_read")

        block = ctx.enter_context(nc.Block())

        @block.sync
        def _(sp):
            for n, (dst, name) in enumerate(((wq_n, "wq1"), (wk_n, "wk1"), (w_t, "ffwt"), (a1_n, "ffa1"), (a2_n, "ffa2"), (wv_t, "wv1t"))):
                sp.dma_start(dst[:, :, :], io[name]).then_inc(fold_in[n // 2] if n < 4 else w_in, 16)
            sp.dma_start(bq[:, :], io["bq"]).then_inc(w_in, 16)
            sp.dma_start(bk[:, :], io["bk"]).then_inc(w_in, 16)
            sp.dma_start(bv[:, :], io["bv"].rearrange("(a c) -> a c", a=1)).then_inc(w_in, 16)
            for n in range(2):
                sp.dma_start(ctxt[n][:, :, :], io["ctxt"][n]).then_inc(ctx_in[n], 16)
            for n in range(2):
                sp.dma_start(wraw[n][:, :, :], io["we"][n]).then_inc(expert_in, 16)
            with sp.Fori(1, B // 2) as i:
                for c in range(2):
                    sp.wait_ge(v_made, 2 * i + (c - 1))
                    sp.dma_start(ctxt[c][:, :, :], io["ctxt"][2 * i + c]).then_inc(ctx_in[c], 16)
            sp.wait_ge(first_slot, 1)
            sp.dma_start(slots_dram.rearrange("e (a b) -> a e b", a=32)[:, 0, :], slot[:, 0, :]).then_inc(slots_stored, 16)
            sp.wait_ge(slots_stored, 16)
            sp.dma_start(slots[:, 0, :], slots_dram.rearrange("e (p q) -> p e q", p=P)[:, 0, :]).then_inc(first_in, 16)
            sp.wait_ge(slot_set, E + 1)
            sp.dma_start(slots_dram.rearrange("e (a b) -> a e b", a=32)[:, 1:, :], slot[:, 1:, :]).then_inc(slots_stored, 16)
            sp.wait_ge(slots_stored, 32)
            sp.wait_ge(expert_in, 32)

        @block.gpsimd
        def _(pool):
            pool.memset(ones[:, :], 1.0).then_inc(ones_set, 1)
            pool.memset(onesf[:, :], 1.0).then_inc(ones_set, 1)
            pool.memset(tri[:, :], 0.0).then_inc(zero_tri, 1)
            pool.wait_ge(zero_tri, 1)
            pool.affine_select(out=tri[:, :], in_=tri[:, :], compare_op=ALU.is_gt, fill=1.0, base=0,
                               pattern=[[-1, P]], channel_multiplier=1).then_inc(tri_set, 1)
            pool.memset(blocks[:, :], 0.0).then_inc(blocks_zero, 1)
            pool.wait_ge(blocks_zero, 1)
            for e in range(4):
                pool.memset(blocks[e * NT:(e + 1) * NT, e * NT:(e + 1) * NT], 1.0).then_inc(blocks_set, 1)
                pool.wait_ge(blocks_set, e + 1)
            pool.iota(iota[:, :], pattern=[[1, 32]], base=0, channel_multiplier=0).then_inc(iota_set, 1)
            pool.iota(row[:, :], pattern=[[0, 1]], base=0, channel_multiplier=1).then_inc(iota_set, 1)
            pool.memset(keep[:, :, :], 1.0).then_inc(consts, 1)
            pool.wait_ge(consts, 1)
            pool.memset(keep[:, :, 0:1], 0.0).then_inc(consts, 1)
            pool.memset(total[:, :, 0:1], 0.0).then_inc(consts, 1)
            pool.wait_ge(iota_set, 2)
            nc.gpsimd.tensor_copy(values_of[:, :, :], iota[:, :].unsqueeze(2).to_broadcast([P, 32, NT])).then_inc(consts, 1)
            nc.gpsimd.tensor_copy(tile_no[:, :], iota[:, :]).then_inc(consts, 1)
            nc.gpsimd.tensor_copy(row_no[:, :], row[:, :]).then_inc(consts, 1)
            pool.wait_ge(max_set, 1)
            nc.gpsimd.partition_all_reduce(expert_max[:, :], pmax[:, :], P, bass.bass_isa.ReduceOp.max).then_inc(max_all, 1)
            for n in range(2):
                pool.wait_ge(expert_hi, n + 1)
                nc.gpsimd.tensor_tensor(up_l[n][:, :, :], wraw[n][:, 0:2, :], up_h[n][:, :, :].bitcast(F32), ALU.subtract).then_inc(expert_lo, 1)
            pool.wait_ge(first_in, 16)
            for q in range(QT):
                pool.indirect_dma_start(out=xg[0][:, q, :], out_offset=None, in_=xn1_dram,
                                        in_offset=bass.IndirectOffsetOnAxis(ap=slots[:, 0, q:q + 1], axis=0)).then_inc(first_gathered, 16)
            pool.wait_ge(first_gathered, 16 * QT)

        @block.tensor
        def _(pe):
            def fold(pairs):
                for out_ap, terms in pairs:
                    for n, (lhs, rhs) in enumerate(terms):
                        last = nc.tensor.matmul(out_ap, lhs, rhs, start=n == 0, stop=n == len(terms) - 1)
                last.then_inc(folded, 1)

            def cols(t):
                return slice(t * P, (t + 1) * P)

            def fold_squares(n):
                lhs, rhs = ((wk_n, wq_n), (a1_n, w_t), (wa_t, a2_n))[n]
                fold([(square_ps[n][:, m * D:(m + 1) * D], [(lhs[:, k, cols(m)], rhs[:, k, :]) for k in range(KD)]) for m in range(KD)])

            def fold_columns():
                fold([(column_ps[:, m:m + 1], [(wq_n[:, k, cols(m)], bk[:, k:k + 1]) for k in range(KD)]) for m in range(KD)]
                     + [(column_ps[:, 2 + m:3 + m], [(wk_n[:, k, cols(m)], bq[:, k:k + 1]) for k in range(KD)]) for m in range(KD)]
                     + [(column_ps[:, 4:5], [(bqb[:, k, :], bk[:, k:k + 1]) for k in range(KD)])])

            def tally(n, c):
                pe.wait_ge(over_set, n + 1)
                nc.tensor.matmul(cnt_ps[c % 2][:, 0:2], blocks[:, :], count2[:, :], start=True, stop=True).then_inc(counted, 1)

            def second_keys(i, c):
                pe.wait_ge(ctx_in[c], 16 * (i + 1))
                if not (isinstance(i, int) and i == 0):
                    pe.wait_ge(m_read, 2 * i + (c - 1))
                for m in range(KD):
                    for k in range(KD):
                        nc.tensor.matmul(m_ps[c][:, m * J:(m + 1) * J], gt[:, k, cols(m)], ctxt[c][:, k, :],
                                         start=k == 0, stop=k == KD - 1)
                for k in range(KD):
                    last = nc.tensor.matmul(m_ps[c][:, 2 * J:3 * J], w2b[:, k, :], ctxt[c][:, k, :], start=k == 0, stop=k == KD - 1)
                last.then_inc(m_made, 1)

            def second_values(i, c):
                if isinstance(i, int) and i == 0:
                    pe.wait_ge(fold_read, 3)
                if not (isinstance(i, int) and i == 0):
                    pe.wait_ge(v_read, 2 * i + (c - 1))
                nc.tensor.matmul(v_ps[c][0:J, 0:D], onesf[0:1, 0:J], bv[0:1, :], start=True, stop=False)
                for k in range(KD):
                    last = nc.tensor.matmul(v_ps[c][0:J, 0:D], ctxt[c][:, k, :], wv_t[:, k, :], start=False, stop=k == KD - 1)
                last.then_inc(v_made, 1)

            for h in range(2):
                last = nc.tensor.transpose(sum_ps[:, h * P:(h + 1) * P],
                                           scores[:, 4 * h:4 * h + 4, :].rearrange("p e t -> p (e t)"), ident[:, :])
            last.then_inc(turn_made, 1)
            pe.wait_ge(blocks_set, 4)
            tally(0, 0)
            tally(1, 1)
            pe.wait_ge(fold_in[0], 32)
            fold_squares(0)
            tally(2, 0)
            pe.wait_ge(fold_in[1], 32)
            fold_squares(1)
            tally(3, 1)
            pe.wait_ge(w_in, 16 * 5)
            pe.wait_ge(bc_set, 1)
            fold_columns()
            pe.wait_ge(fold_read, 2)
            fold_squares(2)
            pe.wait_ge(bc_set, 4)
            pe.wait_ge(ones_set, 2)

            def four_bits(i):
                for c in range(2):
                    tally(4 * i + (2 * c + 4), 0)
                    second_keys(i, c)
                    tally(4 * i + (2 * c + 5), 1)
                    second_values(i, c)

            four_bits(0)
            with pe.Fori(1, B // 2 - 1) as i:
                four_bits(i)

            def prefix(n, src):
                pe.wait_ge(over_set, 32 + n)
                nc.tensor.matmul(cnt_ps[1][:, 0:E * NT], ones[:, :], src, start=True, stop=True)
                nc.tensor.matmul(cnt_ps[0][:, 0:E * NT], tri[:, :], src, start=True, stop=True).then_inc(counted, 1)

            pe.wait_ge(limits_set, 1)
            for h in range(2):
                last = nc.tensor.transpose(fold_ps[:, h * P:(h + 1) * P], limits[:, h, :].bitcast(F32), ident[:, :])
            last.then_inc(counted, 1)
            pe.wait_ge(tri_set, 1)
            pe.wait_ge(over_set, 33)
            nc.tensor.matmul(sum_ps[:, 0:E * NT], ones[:, :], over[:, :, :].rearrange("p e t -> p (e t)"),
                             start=True, stop=True).then_inc(counted, 1)
            prefix(2, equal[:, :, :].rearrange("p e t -> p (e t)"))
            second_keys(B // 2 - 1, 0)
            second_values(B // 2 - 1, 0)
            second_keys(B // 2 - 1, 1)
            prefix(3, chosen[:, :, :].rearrange("p e t -> p (e t)"))
            second_values(B // 2 - 1, 1)
            pe.wait_ge(grown_set, 3)
            nc.tensor.matmul(sum_ps[:, 0:E], onesf[:, :], gsum[:, :], start=True, stop=True).then_inc(counted, 1)
            for e in range(E):
                pe.wait_ge(onehot, 2 * e + 2)
                if e < 2:
                    pe.wait_ge(v_read, B)
                if e >= 2:
                    pe.wait_ge(slot_set, e - 1)
                for t in range(NT):
                    last = nc.tensor.matmul(v_ps[e % 2][0:32, 0:32], A[e % 2][:, :, t],
                                            C[e % 2][:, :, :, t].rearrange("p a b -> p (a b)"), start=t == 0, stop=t == NT - 1)
                last.then_inc(gathered, 1)

        @block.scalar
        def _(act):
            act.wait_ge(w_in, 16 * 5)
            nc.scalar.copy(bqb[:, :, :], bq[:, :].unsqueeze(2).to_broadcast([P, KD, P])).then_inc(bc_set, 1)
            for n, dst in enumerate((gt, wa_t)):
                act.wait_ge(folded, n + 1)
                nc.scalar.copy(dst[:, :, :].rearrange("p a b -> p (a b)"), square_ps[n][:, :]).then_inc(fold_read, 1)
            act.wait_ge(folded, 3)
            nc.scalar.copy(w2b[:, :, :], column_ps[:, 2:4].unsqueeze(2).to_broadcast([P, KD, P])).then_inc(bc_set, 1)
            nc.scalar.copy(u[:, :], column_ps[:, 0:2]).then_inc(bc_set, 1)
            nc.scalar.mul(s0[:, :], column_ps[:, 4:5], D ** -0.5).then_inc(bc_set, 1)
            act.wait_ge(folded, 4)
            nc.scalar.copy(ffn_w[:, :, :].rearrange("p a b -> p (a b)"), square_ps[2][:, :]).then_inc(fold_read, 1)
            act.wait_ge(bc_set, 4)

            def read(i, c):
                act.wait_ge(m_made, 2 * i + (c + 1))
                b = 2 * i + c
                for m in range(KD):
                    nc.scalar.activation(keys_m[:, bass.ds(KD * b + m, 1), :].rearrange("p a j -> p (a j)"), m_ps[c][:, m * J:(m + 1) * J], ACT.Identity, bias=u[:, m:m + 1])
                nc.scalar.activation(keys_bias[:, bass.ds(b, 1), :].rearrange("p a j -> p (a j)"), m_ps[c][:, 2 * J:3 * J], ACT.Identity, scale=D ** -0.5,
                                     bias=s0[:, 0:1]).then_inc(m_read, 1)
                act.wait_ge(v_made, 2 * i + (c + 1))
                nc.scalar.copy(values[:, bass.ds(b, 1), :].rearrange("p a j -> p (a j)"), v_ps[c][0:J, 0:D]).then_inc(v_read, 1)

            with act.Fori(0, B // 2) as i:
                for c in range(2):
                    read(i, c)
            act.wait_ge(grown_set, 1)
            nc.scalar.activation(grown[:, :, :], grown[:, :, :], ACT.Exp).then_inc(grown_set, 1)
            act.wait_ge(expert_in, 32)
            for n in range(2):
                nc.scalar.copy(up_h[n][:, :, :], wraw[n][:, 0:2, :]).then_inc(expert_hi, 1)

        @block.vector
        def _(dve):
            V = nc.vector
            done = [0]

            def then(ins):
                done[0] += 1
                ins.then_inc(step_done, 1)
                dve.wait_ge(step_done, done[0])

            V.memset(bits[1][:, :], 1).then_inc(bit_set, 1)
            V.memset(cand[:, :], 0).then_inc(cand_set, 1)
            dve.wait_ge(turn_made, 1)
            V.tensor_copy(turned[:, :, :].rearrange("p h r -> p (h r)"), sum_ps[:, 0:2 * P]).then_inc(turn_read, 1)
            dve.wait_ge(turn_read, 1)

            def reach(n):
                dve.wait_ge(cand_set, n + 1)
                for h in range(2):
                    last = V.tensor_scalar(reached[:, h, :], turned[:, h, :], cand[:, h:h + 1].bitcast(F32), 0.0,
                                           ALU.is_ge, ALU.add, accum_out=count2[:, h:h + 1])
                last.then_inc(over_set, 1)

            reach(0)
            dve.wait_ge(bit_set, 1)
            V.tensor_scalar(bits[1][:, :], bits[1][:, :], 30, None, ALU.logical_shift_left).then_inc(bit_set, 1)
            dve.wait_ge(counted, 1)
            V.tensor_scalar(back[:, :], cnt_ps[0][:, 0:2], CAP - 0.5, float(1 << 31), ALU.is_lt, ALU.mult).then_inc(back_set, 1)
            dve.wait_ge(back_set, 1)
            V.tensor_scalar(flipped[:, :], back[:, :], 31, None, ALU.arith_shift_right).then_inc(flip_set, 1)
            dve.wait_ge(flip_set, 1)
            dve.wait_ge(bit_set, 2)
            V.tensor_tensor(cand[:, :], flipped[:, :], bits[1][:, :], ALU.bitwise_xor).then_inc(cand_set, 1)

            def one_bit(n, c):
                now, following = bits[c % 2], bits[(c + 1) % 2]
                reach(n)
                V.tensor_scalar(following[:, :], now[:, :], 1, None, ALU.logical_shift_right).then_inc(bit_set, 1)
                dve.wait_ge(bit_set, n + 2)
                V.tensor_tensor(flipped[:, :], cand[:, :], following[:, :], ALU.bitwise_xor).then_inc(flip_set, 1)
                dve.wait_ge(counted, n + 1)
                V.scalar_tensor_tensor(out=back[:, :], in0=cnt_ps[c % 2][:, 0:2], scalar=CAP - 0.5, in1=now[:, :],
                                       op0=ALU.is_lt, op1=ALU.mult).then_inc(back_set, 1)
                dve.wait_ge(back_set, n + 1)
                dve.wait_ge(flip_set, n + 1)
                V.tensor_tensor(cand[:, :], flipped[:, :], back[:, :], ALU.bitwise_xor).then_inc(cand_set, 1)

            for n in range(1, 4):
                one_bit(n, n)
            with dve.Fori(1, 8) as i:
                for c in range(4):
                    one_bit(4 * i + c, c)

            dve.wait_ge(cand_set, 33)
            V.tensor_copy(limits[:, :, :], cand[:, :].unsqueeze(2).to_broadcast([P, 2, P])).then_inc(limits_set, 1)
            V.tensor_reduce(pmax[:, :], scores[:, :, :], AX.X, ALU.max).then_inc(max_set, 1)
            dve.wait_ge(counted, 33)
            least = fold_ps[:, 0:E * NT].rearrange("p (e t) -> p e t", e=E)
            V.tensor_tensor(over[:, :, :], scores[:, :, :], least, ALU.is_gt).then_inc(over_set, 1)
            V.tensor_tensor(equal[:, :, :], scores[:, :, :], least, ALU.is_equal).then_inc(over_set, 1)
            dve.wait_ge(consts, 6)
            dve.wait_ge(counted, 34)
            then(V.tensor_reduce(count[:, :], sum_ps[:, 0:E * NT].rearrange("p (e t) -> p e t", e=E), AX.X, ALU.add))
            then(V.tensor_scalar(need[:, :], count[:, :], -1.0, float(CAP), ALU.mult, ALU.add))

            def up_to(dst):
                then(V.tensor_copy(total[:, :, 1:], cnt_ps[1][:, 0:E * NT].rearrange("p (e t) -> p e t", e=E)[:, :, 0:NT - 1]))
                then(V.tensor_tensor_scan(dst[:, :, :].rearrange("p e t -> p (e t)"), keep[:, :, :].rearrange("p e t -> p (e t)"),
                                          total[:, :, :].rearrange("p e t -> p (e t)"), 0.0, ALU.mult, ALU.add))
                then(V.tensor_tensor(dst[:, :, :].rearrange("p e t -> p (e t)"), cnt_ps[0][:, 0:E * NT],
                                     dst[:, :, :].rearrange("p e t -> p (e t)"), ALU.add))

            dve.wait_ge(counted, 35)
            up_to(rank)
            then(V.tensor_tensor(rank[:, :, :], rank[:, :, :], need[:, :].unsqueeze(2).to_broadcast(wide), ALU.is_le))
            then(V.tensor_tensor(rank[:, :, :], rank[:, :, :], equal[:, :, :], ALU.mult))
            V.tensor_tensor(chosen[:, :, :], rank[:, :, :], over[:, :, :], ALU.add).then_inc(over_set, 1)
            dve.wait_ge(max_all, 1)
            V.tensor_tensor(grown[:, :, :], scores[:, :, :], expert_max[:, :].unsqueeze(2).to_broadcast(wide),
                            ALU.subtract).then_inc(grown_set, 1)
            dve.wait_ge(counted, 36)
            up_to(place)
            then(V.tensor_tensor(place[:, :, :], place[:, :, :], chosen[:, :, :], ALU.mult))
            then(V.tensor_scalar(whole[:, :, :], place[:, :, :], -1.0, None, ALU.add))
            V.tensor_scalar(place_lo[:, :, :].bitcast(I32), whole[:, :, :], 15, None, ALU.bitwise_and).then_inc(ranked, 1)
            V.tensor_scalar(place_hi[:, :, :].bitcast(I32), whole[:, :, :], 4, None, ALU.arith_shift_right).then_inc(ranked, 1)
            dve.wait_ge(ranked, 2)
            V.tensor_copy(low[:, :, :], place_lo[:, :, :].bitcast(I32)).then_inc(ranked, 1)
            V.tensor_copy(high[:, :, :], place_hi[:, :, :].bitcast(I32)).then_inc(ranked, 1)
            dve.wait_ge(grown_set, 2)
            then(V.tensor_tensor(grown[:, :, :], grown[:, :, :], chosen[:, :, :], ALU.mult))
            V.tensor_reduce(gsum[:, :], grown[:, :, :], AX.X, ALU.add).then_inc(grown_set, 1)
            dve.wait_ge(counted, 37)
            then(V.tensor_copy(count[:, :], sum_ps[:, 0:E]))
            V.reciprocal(expert_inv[:, :], count[:, :])
            dve.wait_ge(ranked, 4)

            def read_slots(e):
                dve.wait_ge(gathered, e + 1)
                V.tensor_copy(slotf[:, e, :, :].rearrange("p a b -> p (a b)"), v_ps[e % 2][0:32, 0:32]).then_inc(slot_set, 1)
                if e == 0:
                    dve.wait_ge(slot_set, 1)
                    V.scalar_tensor_tensor(out=slot[:, 0, :], in0=slotf[:, 0, 0, :], scalar=float(P), in1=slotf[:, 0, 1, :],
                                           op0=ALU.mult, op1=ALU.add).then_inc(first_slot, 1)

            for e in range(E):
                if e >= 2:
                    dve.wait_ge(gathered, e - 1)
                then(V.tensor_tensor(C[e % 2][:, 1, :, :], low[:, e, :].unsqueeze(1).to_broadcast([P, 16, NT]),
                                     values_of[:, 0:16, :], ALU.is_equal))
                V.tensor_tensor(A[e % 2][:, :, :], high[:, e, :].unsqueeze(1).to_broadcast([P, 32, NT]),
                                values_of[:, :, :], ALU.is_equal).then_inc(onehot, 1)
                then(V.tensor_tensor(C[e % 2][:, 0, :, :], C[e % 2][:, 1, :, :],
                                     tile_no[:, :].unsqueeze(1).to_broadcast([P, 16, NT]), ALU.mult))
                V.tensor_scalar(C[e % 2][:, 1, :, :], C[e % 2][:, 1, :, :], row_no[:, 0:1], None, ALU.mult).then_inc(onehot, 1)
                if e >= 1:
                    read_slots(e - 1)
            read_slots(E - 1)
            dve.wait_ge(slot_set, E)
            V.scalar_tensor_tensor(out=slot[:, 1:, :], in0=slotf[:, 1:, 0, :], scalar=float(P), in1=slotf[:, 1:, 1, :],
                                   op0=ALU.mult, op1=ALU.add).then_inc(slot_set, 1)


def expert_loop(eng, body):
    for c in range(2):
        body(0, c)
    with eng.Fori(1, E // 2 - 1) as i:
        for c in range(2):
            body(i, c)
    for c in range(2):
        body(E // 2 - 1, c)


def experts(nc, io, x1_dram, xn1_dram, slots_dram, ident, expert_max, expert_inv, weights, slots, xg, outer):
    wraw, up_h, up_l, down_h, down_l = weights
    with ExitStack() as ctx:
        def sb(name, shape, dt=F32):
            return ctx.enter_context(nc.sbuf_tensor("e_" + name, shape, dt))

        def ps(name):
            return ctx.enter_context(nc.psum_tensor("ep_" + name, [P, 512], F32))

        def sem(name):
            return ctx.enter_context(nc.semaphore("e_" + name))

        wg = sb("wg", [P, E, D])
        xgh = sb("xgh", [P, KD, CAP], F32R)
        xgl = sb("xgl", [P, KD, CAP], F32R)
        prod = sb("prod", [P, D])
        gate = [sb(f"gate{n}", [P, QT]) for n in range(2)]
        weight = [sb(f"weight{n}", [P, QT]) for n in range(2)]
        negmax = sb("negmax", [P, E])
        halfinv = sb("halfinv", [P, E])
        hid = [sb(f"hid{n}", [P, CAP]) for n in range(2)]
        hh = [sb(f"hh{n}", [P, HT, CAP], F32R) for n in range(2)]
        hl = [sb(f"hl{n}", [P, HT, CAP], F32R) for n in range(2)]
        y = [sb(f"y{n}", [P, QT, D]) for n in range(2)]

        t_ps = [ps("t0"), ps("t1")]
        u_ps = [ps("u0"), ps("u1")]
        g_ps = [ps("g0"), ps("g1")]
        y_ps = [ps("y0"), ps("y1")]

        mark = sb("mark", [P, E + 1])
        small_in, slots_in = sem("small_in"), sem("slots_in")
        w_in = [sem(f"w_in{n}") for n in range(2)]
        up_hi, up_lo, down_hi, down_lo = sem("up_hi"), sem("up_lo"), sem("down_hi"), sem("down_lo")
        x_in = [sem(f"x_in{n}") for n in range(2)]
        added = [sem(f"added{n}") for n in range(2)]
        y_free = [sem(f"y_free{n}") for n in range(2)]
        signs, gates_done, exped, weighted = sem("signs"), sem("gates_done"), sem("exped"), sem("weighted")
        t_made, t_hi, t_lo = sem("t_made"), sem("t_hi"), sem("t_lo")
        up_made, tanh_done, gated_done, hid_done, h_hi, h_lo = (sem(n) for n in ("up_made", "tanh_done", "gated_done", "hid_done", "h_hi", "h_lo"))
        y_made, y_done = sem("y_made"), sem("y_done")

        second_sems = [outer.enter_context(nc.semaphore("l_" + name)) for name in SECOND_SEMAPHORES]

        block = ctx.enter_context(nc.Block())

        @block.sync
        def _(sp):
            sp.dma_start(slots[:, 1:, :], slots_dram.rearrange("e (p q) -> p e q", p=P)[:, 1:, :]).then_inc(slots_in, 16)
            sp.dma_start(wg[:, :, :].rearrange("p e c -> p (e c)"), io["wg"].rearrange("(a e) c -> a (e c)", a=1).to_broadcast([P, E * D])).then_inc(small_in, 16)

            def load(i, c):
                sp.dma_start(wraw[c][:, :, :], io["we"][2 * i + c]).then_inc(w_in[c], 16)

            with sp.Fori(1, E // 2) as i:
                for c in range(2):
                    sp.wait_ge(down_lo, 2 * i + (c - 1))
                    load(i, c)

        @block.gpsimd
        def _(pool):
            def gather(i, c):
                e = 2 * i + c
                for q in range(QT):
                    pool.indirect_dma_start(out=xg[c][:, q, :], out_offset=None, in_=xn1_dram,
                                            in_offset=bass.IndirectOffsetOnAxis(ap=slots[:, e, q:q + 1], axis=0)).then_inc(x_in[c], 16)

            def scatter(e):
                c = e % 2
                if e >= 1:
                    pool.wait_ge(added[1 - c], 16 * QT * ((e - 1) // 2 + 1))
                    pool.memset(mark[:, e + 1:e + 2], 0.0).then_inc(y_free[1 - c], 1)
                for q in range(QT):
                    if q % 2 == 0:
                        pool.wait_ge(y_done, 2 * e + q // 2 + 1)
                    pool.indirect_dma_start(out=x1_dram, out_offset=bass.IndirectOffsetOnAxis(ap=slots[:, e, q:q + 1], axis=0),
                                            in_=y[c][:, q, :], in_offset=None, compute_op=ALU.add).then_inc(added[c], 16)

            for c in range(2):
                pool.memset(mark[:, c:c + 1], 0.0).then_inc(y_free[c], 1)
            pool.wait_ge(slots_in, 16)
            gather(0, 1)
            for s in second_sems:
                pool.sem_clear(s)
            for e in range(E):
                if e + 2 < E:
                    pool.wait_ge(t_made, 2 * (e + 1))
                    pool.wait_ge(gates_done, QT * (e + 1))
                    gather(e // 2 + 1, e % 2)
                if e >= 1:
                    scatter(e - 1)
            scatter(E - 1)
            pool.wait_ge(added[1], 16 * QT * (E // 2))

        @block.tensor
        def _(pe):
            def mm3(out_ap, lhs, rhs, start, stop):
                (lh, ll), (rh, rl) = lhs, rhs
                nc.tensor.matmul(out_ap, lh, rh, start=start, stop=False)
                nc.tensor.matmul(out_ap, lh, rl, start=False, stop=False)
                return nc.tensor.matmul(out_ap, ll, rh, start=False, stop=stop)

            def turn(i, c):
                e = 2 * i + c
                if not (isinstance(e, int) and e == 0):
                    pe.wait_ge(x_in[c], 16 * QT * (i + c))
                for k in range(KD):
                    if not (isinstance(e, int) and e == 0):
                        pe.wait_ge(t_lo, 2 * e - 1 + k)
                    for q in range(QT):
                        last = nc.tensor.transpose(t_ps[k][:, q * P:(q + 1) * P], xg[c][:, q, k * P:(k + 1) * P], ident[:, :])
                    last.then_inc(t_made, 1)

            def up(i, c):
                e = 2 * i + c
                pe.wait_ge(t_hi, 2 * e + 2)
                pe.wait_ge(t_lo, 2 * e + 2)
                if not (isinstance(e, int) and e < 2):
                    pe.wait_ge(up_hi, 2 * e - 2)
                    pe.wait_ge(up_lo, 2 * e - 2)
                for m in range(HT):
                    if not (isinstance(e, int) and e == 0 and m < 2):
                        pe.wait_ge(hid_done, HT * e + m - 1)
                    for bank, w in ((u_ps[m % 2], 0), (g_ps[m % 2], 1)):
                        for k in range(KD):
                            cols = slice(k * HID + m * P, k * HID + (m + 1) * P)
                            last = mm3(bank[:, :], (up_h[c][:, w, cols], up_l[c][:, w, cols]), (xgh[:, k, :], xgl[:, k, :]),
                                       k == 0, k == KD - 1)
                        last.then_inc(up_made, 1)

            def down(e, c):
                pe.wait_ge(h_hi, HT * e + HT)
                pe.wait_ge(h_lo, HT * e + HT)
                pe.wait_ge(down_hi, e + 1)
                pe.wait_ge(down_lo, e + 1)
                for q in range(QT):
                    if not (isinstance(e, int) and e == 0) and q % 2 == 0:
                        pe.wait_ge(y_done, 2 * e - 1 + q // 2)
                    for m in range(HT):
                        rows, cols = slice(q * P, (q + 1) * P), slice(m * D, (m + 1) * D)
                        last = mm3(y_ps[q // 2][:, (q % 2) * D:(q % 2 + 1) * D], (hh[c][:, m, rows], hl[c][:, m, rows]),
                                   (down_h[c][:, cols], down_l[c][:, cols]), m == 0, m == HT - 1)
                    if q % 2:
                        last.then_inc(y_made, 1)

            turn(0, 0)

            def body(i, c):
                up(i, c)
                if c == 0:
                    turn(i, 1)
                elif not (isinstance(i, int) and i == E // 2 - 1):
                    turn(i + 1, 0)
                if c == 1:
                    down(2 * i, 0)
                elif not (isinstance(i, int) and i == 0):
                    down(2 * i - 1, 1)

            expert_loop(pe, body)
            down(E - 1, 1)

        @block.scalar
        def _(act):
            def leading(i, c):
                e = 2 * i + c
                for k in range(KD):
                    act.wait_ge(t_made, 2 * e + k + 1)
                    if not (isinstance(e, int) and e == 0) and k == 0:
                        act.wait_ge(up_made, 2 * HT * e)
                    nc.scalar.copy(xgh[:, k, :], t_ps[k][:, :]).then_inc(t_hi, 1)

            def outputs(i, c):
                e = 2 * i + c
                act.wait_ge(weighted, e + 1)
                act.wait_ge(y_free[c], i + 1)
                for n in range(2):
                    act.wait_ge(y_made, 2 * e + (n + 1))
                    for q in (2 * n, 2 * n + 1):
                        last = nc.scalar.mul(y[c][:, q, :], y_ps[n][:, (q % 2) * D:(q % 2 + 1) * D], weight[c][:, q:q + 1])
                    last.then_inc(y_done, 1)

            leading(0, 0)

            def body(i, c):
                e = 2 * i + c
                there = not (isinstance(i, int) and i == E // 2 - 1 and c == 1)
                for m in range(HT):
                    act.wait_ge(up_made, 2 * HT * e + (2 * m + 1))
                    if not (isinstance(e, int) and e == 0 and m < 2):
                        act.wait_ge(h_lo, HT * e + (m - 1))
                    nc.scalar.activation(hid[m % 2][:, :], u_ps[m % 2][:, :], ACT.Tanh, scale=0.5).then_inc(tanh_done, 1)
                    if m == 0:
                        nc.scalar.copy(down_h[c][:, :], wraw[c][:, 2, :]).then_inc(down_hi, 1)
                    if m in (1, 2) and there and not (isinstance(e, int) and e == 0):
                        if m == 1:
                            act.wait_ge(w_in[1 - c], 16 * (i + c))
                        nc.scalar.copy(up_h[1 - c][:, m - 1, :], wraw[1 - c][:, m - 1, :]).then_inc(up_hi, 1)
                    act.wait_ge(hid_done, HT * e + (m + 1))
                    if not (isinstance(i, int) and i == 0) and m == 0:
                        act.wait_ge(y_made, 2 * e - 2)
                    nc.scalar.copy(hh[c][:, m, :], hid[m % 2][:, :]).then_inc(h_hi, 1)
                if there:
                    leading(*((i, 1) if c == 0 else (i + 1, 0)))
                if c == 1:
                    outputs(i, 0)
                elif not (isinstance(i, int) and i == 0):
                    outputs(i - 1, 1)
                act.wait_ge(gates_done, QT * e + QT)
                if not (isinstance(i, int) and i == 0):
                    act.wait_ge(y_done, 2 * e - 2)
                nc.scalar.activation(weight[c][:, :], gate[c][:, :], ACT.Exp, bias=negmax[:, bass.ds(e, 1)]).then_inc(exped, 1)

            expert_loop(act, body)
            outputs(E // 2 - 1, 1)

        @block.vector
        def _(dve):
            V = nc.vector
            V.tensor_scalar(negmax[:, :], expert_max[:, :], -1.0, None, ALU.mult).then_inc(signs, 1)
            V.tensor_scalar(halfinv[:, :], expert_inv[:, :], 0.5, None, ALU.mult).then_inc(signs, 1)

            def score(i, c):
                e = 2 * i + c
                if not (isinstance(e, int) and e == 0):
                    dve.wait_ge(x_in[c], 16 * QT * (i + c))
                if not (isinstance(i, int) and i == 0):
                    dve.wait_ge(exped, e - 1)
                for q in range(QT):
                    if not (isinstance(e, int) and e == 0 and q == 0):
                        dve.wait_ge(gates_done, QT * e + q)
                    V.scalar_tensor_tensor(out=prod[:, :], in0=xg[c][:, q, :], scalar=1.0,
                                           in1=wg[:, bass.ds(e, 1), :].rearrange("p a c -> p (a c)"),
                                           op0=ALU.mult, op1=ALU.mult, accum_out=gate[c][:, q:q + 1]).then_inc(gates_done, 1)

            def rest(i, c):
                e = 2 * i + c
                for k in range(KD):
                    dve.wait_ge(t_hi, 2 * e + (k + 1))
                    V.tensor_tensor(xgl[:, k, :], t_ps[k][:, :], xgh[:, k, :].bitcast(F32), ALU.subtract).then_inc(t_lo, 1)

            def weigh(e, c):
                dve.wait_ge(exped, e + 1)
                V.tensor_scalar(weight[c][:, :], weight[c][:, :], halfinv[:, bass.ds(e, 1)], None, ALU.mult).then_inc(weighted, 1)

            rest(0, 0)

            def body(i, c):
                e = 2 * i + c
                there = not (isinstance(i, int) and i == E // 2 - 1 and c == 1)
                if c == 1:
                    weigh(2 * i, 0)
                elif not (isinstance(i, int) and i == 0):
                    weigh(2 * i - 1, 1)
                for m in range(HT):
                    dve.wait_ge(tanh_done, HT * e + (m + 1))
                    V.scalar_tensor_tensor(out=hid[m % 2][:, :], in0=hid[m % 2][:, :], scalar=1.0, in1=u_ps[m % 2][:, :],
                                           op0=ALU.add, op1=ALU.mult).then_inc(gated_done, 1)
                    dve.wait_ge(gated_done, HT * e + (m + 1))
                    dve.wait_ge(up_made, 2 * HT * e + (2 * m + 2))
                    V.tensor_tensor(hid[m % 2][:, :], hid[m % 2][:, :], g_ps[m % 2][:, :], ALU.mult).then_inc(hid_done, 1)
                    if m == 1:
                        dve.wait_ge(down_hi, e + 1)
                        V.tensor_tensor(down_l[c][:, :], wraw[c][:, 2, :], down_h[c][:, :].bitcast(F32), ALU.subtract).then_inc(down_lo, 1)
                    if m >= 2 and there and not (isinstance(e, int) and e == 0):
                        dve.wait_ge(up_hi, 2 * e + (m - 3))
                        V.tensor_tensor(up_l[1 - c][:, m - 2, :], wraw[1 - c][:, m - 2, :], up_h[1 - c][:, m - 2, :].bitcast(F32),
                                        ALU.subtract).then_inc(up_lo, 1)
                    dve.wait_ge(h_hi, HT * e + (m + 1))
                    V.tensor_tensor(hl[c][:, m, :], hid[m % 2][:, :], hh[c][:, m, :].bitcast(F32), ALU.subtract).then_inc(h_lo, 1)
                if there:
                    after = (i, 1) if c == 0 else (i + 1, 0)
                    rest(*after)
                if isinstance(e, int) and e == 0:
                    dve.wait_ge(small_in, 16)
                    dve.wait_ge(signs, 2)
                score(i, c)

            expert_loop(dve, body)
            weigh(E - 1, 1)

        return second_sems


def second_layer(nc, io, x2_dram, out_dram, ident, second, sems):
    _, keys_m, keys_bias, values, ffn_w = second
    SC = D ** -0.5
    with ExitStack() as ctx:
        def sb(name, shape, dt=F32):
            return ctx.enter_context(nc.sbuf_tensor("l_" + name, shape, dt))

        def ps(name):
            return ctx.enter_context(nc.psum_tensor("lp_" + name, [P, 512], F32))

        def sem(name):
            return sems[SECOND_SEMAPHORES.index(name)]

        x2 = [sb(f"x2{n}", [P, TT, D]) for n in range(4)]
        side = [sb(f"side{n}", [P, TT, J]) for n in range(2)]
        betas = sb("betas", [P, 3])
        neghalf = sb("neghalf", [P, TT])
        coef = sb("coef", [P, 1])
        bias_w = sb("bias_w", [P, D])
        sided = [sb(f"sided{n}", [P, TT, J]) for n in range(2)]
        bn = [sb(f"bn{n}", [P, TT, 6]) for n in range(2)]
        turnstile = [sb(f"turnstile{n}", [P, 1]) for n in range(2)]
        mv = [sb(f"mv{n}", [P, TT, 2]) for n in range(2)]
        var = [sb(f"var{n}", [P, TT]) for n in range(2)]
        rstd = [sb(f"rstd{n}", [P, TT]) for n in range(2)]
        xn = [sb(f"xn{n}", [P, TT, D]) for n in range(2)]
        xt = [sb(f"xt{n}", [P, KD, S]) for n in range(2)]
        att = [sb(f"att{n}", [P, TT, J]) for n in range(2)]
        negmax = sb("negmax", [P, TT])
        den = sb("den", [P, TT])
        rden = sb("rden", [P, TT])
        pt = sb("pt", [J, S])
        x3 = [sb(f"x3{n}", [P, TT, D]) for n in range(4)]
        pre = sb("pre", [P, TT, D])
        res = [sb(f"res{n}", [P, TT, D]) for n in range(2)]

        xt_ps = [ps("xt0"), ps("xt1")]
        sim_ps, pt_ps, pv_ps, ff_ps = ps("sim"), ps("pt"), ps("pv"), ps("ff")

        small_in = sem("small_in")
        x_in = [sem(f"x_in{n}") for n in range(4)]
        side_in = [sem(f"side_in{n}") for n in range(2)]
        pre_set = sem("pre_set")
        coef_set, sided_a, sided_b = sem("coef_set"), sem("sided_a"), sem("sided_b")
        bn_done = [sem("bn0"), sem("bn1")]
        mv_done = [sem("mv0"), sem("mv1")]
        var_done = [sem("var0"), sem("var1")]
        half_set = sem("half_set")
        rstd_done = [sem("rstd0"), sem("rstd1")]
        xn_done = [sem("xn0"), sem("xn1")]
        xt_made = [sem("xt_made0"), sem("xt_made1")]
        xt_out = [sem("xt_out0"), sem("xt_out1")]
        sim_made, att_done, max_done, exped, inverted = sem("sim_made"), sem("att_done"), sem("max_done"), sem("exped"), sem("inverted")
        pt_made, pt_out, pv_made, x3_done = sem("pt_made"), sem("pt_out"), sem("pv_made"), sem("x3_done")
        ff_made, pre_done, tanh_done, res_done = sem("ff_made"), sem("pre_done"), sem("tanh_done"), sem("res_done")
        stored = [sem(f"stored{n}") for n in range(2)]

        x2_view = x2_dram.rearrange("(b t p) c -> b p t c", p=P, t=TT)
        out_view = out_dram.rearrange("b (t p) c -> b p t c", p=P)
        side_view = io["fside"].rearrange("b (t p) j -> b p t j", p=P)
        flat = "p a b -> p (a b)"

        def loop(eng, body, lags):
            for n in range(8):
                body(Batch4(0, n))
            with eng.Fori(2, B // 4) as i:
                for c in range(4):
                    body(Batch4(i, c))
            for n in range(B, B + lags):
                body(Batch4(0, n))

        block = ctx.enter_context(nc.Block())
        LAGS = 5

        @block.sync
        def _(sp):
            def loads(b):
                if b.at_least(4):
                    sp.wait_ge(x3_done, b.n - 3)
                sp.dma_start(x2[b.c % 4][:, :, :], x2_view[b.n]).then_inc(x_in[b.c % 4], 16)
                if b.at_least(2):
                    sp.wait_ge(sided_a, b.n - 1)
                sp.dma_start(side[b.c % 2][:, :, :], side_view[b.n]).then_inc(side_in[b.c % 2], 16)

            def body(n):
                if n.real():
                    loads(n)
                if not n.at_least(1):
                    sp.dma_start(betas[:, :], io["betas"].unsqueeze(0).to_broadcast([P, 3])).then_inc(small_in, 16)
                    sp.dma_start(bias_w[:, :], io["ffb"].unsqueeze(0).to_broadcast([P, D])).then_inc(small_in, 16)
                b = n.shift(-5)
                if b.real():
                    sp.wait_ge(res_done, b.n + 1)
                    sp.dma_start(out_view[b.n], res[b.c % 2][:, :, :]).then_inc(stored[b.c % 2], 16)

            loop(sp, body, LAGS)
            for n in range(2):
                sp.wait_ge(stored[n], 16 * (B // 2))

        @block.tensor
        def _(pe):
            def transposes(which, b):
                pe.wait_ge(xn_done[which], b.n + 1)
                if b.at_least(1):
                    pe.wait_ge(xt_out[which], b.n)
                for t in range(TT):
                    for k in range(KD):
                        last = nc.tensor.transpose(xt_ps[which][:, k * S + t * P:k * S + (t + 1) * P],
                                                   xn[which][:, t, k * P:(k + 1) * P], ident[:, :])
                last.then_inc(xt_made[which], 1)

            def scores(b):
                pe.wait_ge(xt_out[0], b.n + 1)
                if b.at_least(1):
                    pe.wait_ge(att_done, b.n)
                for t in range(TT):
                    for k in range(KD):
                        last = nc.tensor.matmul(sim_ps[:, t * J:(t + 1) * J], xt[0][:, k, t * P:(t + 1) * P],
                                                keys_m[:, bass.ds(KD * b.n + k, 1), :].rearrange("p a j -> p (a j)"), start=k == 0, stop=k == KD - 1)
                last.then_inc(sim_made, 1)

            def attention(b):
                pe.wait_ge(exped, b.n + 1)
                if b.at_least(1):
                    pe.wait_ge(pt_out, b.n)
                for t in range(TT):
                    last = nc.tensor.transpose(pt_ps[0:J, t * P:(t + 1) * P], att[b.c % 2][:, t, :], ident[:, :])
                last.then_inc(pt_made, 1)

            def mix(b):
                pe.wait_ge(pt_out, b.n + 1)
                if b.at_least(1):
                    pe.wait_ge(x3_done, b.n)
                for t in range(TT):
                    last = nc.tensor.matmul(pv_ps[:, t * D:(t + 1) * D], pt[:, t * P:(t + 1) * P],
                                            values[:, bass.ds(b.n, 1), :].rearrange("p a c -> p (a c)"), start=True, stop=True)
                last.then_inc(pv_made, 1)

            def feed(b):
                pe.wait_ge(xt_out[1], b.n + 1)
                if b.at_least(1):
                    pe.wait_ge(pre_done, b.n)
                for t in range(TT):
                    for k in range(KD):
                        last = nc.tensor.matmul(ff_ps[:, t * D:(t + 1) * D], xt[1][:, k, t * P:(t + 1) * P], ffn_w[:, k, :],
                                                start=k == 0, stop=k == KD - 1)
                last.then_inc(ff_made, 1)

            def body(n):
                if n.shift(-2).real():
                    scores(n.shift(-2))
                if n.shift(-3).real():
                    attention(n.shift(-3))
                if n.shift(-5).real():
                    feed(n.shift(-5))
                if n.shift(-3).real():
                    mix(n.shift(-3))
                if n.shift(-1).real():
                    transposes(0, n.shift(-1))
                if n.shift(-4).real():
                    transposes(1, n.shift(-4))

            loop(pe, body, LAGS)

        @block.scalar
        def _(act):
            act.wait_ge(coef_set, 1)

            def sides(b):
                act.wait_ge(side_in[b.c % 2], 16 * (b.turn(2) + 1))
                if b.at_least(2):
                    act.wait_ge(att_done, b.n - 1)
                nc.scalar.mul(sided[b.c % 2][:, :, :], side[b.c % 2][:, :, :], coef[:, 0:1]).then_inc(sided_a, 1)

            def xt_copy(which, b):
                act.wait_ge(xt_made[which], b.n + 1)
                if b.at_least(1):
                    act.wait_ge(sim_made if which == 0 else ff_made, b.n)
                nc.scalar.copy(xt[which][:, :, :].rearrange(flat), xt_ps[which][:, :]).then_inc(xt_out[which], 1)

            def exps(b):
                act.wait_ge(max_done, b.n + 1)
                if b.at_least(1):
                    act.wait_ge(inverted, b.n)
                for t in range(TT):
                    last = nc.scalar.activation(att[b.c % 2][:, t, :], att[b.c % 2][:, t, :], ACT.Exp, bias=negmax[:, t:t + 1],
                                                accum_out=den[:, t:t + 1])
                last.then_inc(exped, 1)

            def pt_copy(b):
                act.wait_ge(pt_made, b.n + 1)
                if b.at_least(1):
                    act.wait_ge(pv_made, b.n)
                nc.scalar.copy(pt[:, :], pt_ps[0:J, 0:S]).then_inc(pt_out, 1)

            def tanh(b):
                act.wait_ge(pre_done, b.n + 1)
                nc.scalar.activation(pre[:, :, :], pre[:, :, :], ACT.Tanh).then_inc(tanh_done, 1)

            def body(n):
                if n.shift(-3).real():
                    pt_copy(n.shift(-3))
                if n.shift(-2).real():
                    exps(n.shift(-2))
                if n.shift(-5).real():
                    tanh(n.shift(-5))
                if n.shift(-1).real():
                    xt_copy(0, n.shift(-1))
                if n.shift(-4).real():
                    xt_copy(1, n.shift(-4))
                if n.real():
                    sides(n)

            loop(act, body, LAGS)

        @block.gpsimd
        def _(pool):
            pool.memset(neghalf[:, :], -0.5).then_inc(half_set, 1)
            pool.wait_ge(half_set, 1)

            def rsqrt(which, b):
                pool.wait_ge(var_done[which], b.n + 1)
                nc.gpsimd.tensor_tensor(rstd[which][:, :], var[which][:, :], neghalf[:, :], ALU.pow).then_inc(rstd_done[which], 1)

            def add_keys(b):
                pool.wait_ge(sided_a, b.n + 1)
                nc.gpsimd.tensor_tensor(sided[b.c % 2][:, :, :], sided[b.c % 2][:, :, :],
                                        keys_bias[:, bass.ds(b.n, 1), :].to_broadcast([P, TT, J]), ALU.add).then_inc(sided_b, 1)

            def finish(b):
                pool.wait_ge(tanh_done, b.n + 1)
                if b.at_least(2):
                    pool.wait_ge(stored[b.c % 2], 16 * b.turn(2))
                nc.gpsimd.tensor_tensor(res[b.c % 2][:, :, :], pre[:, :, :], x3[b.c % 4][:, :, :], ALU.add).then_inc(res_done, 1)

            def body(n):
                if n.shift(-5).real():
                    finish(n.shift(-5))
                if n.real():
                    rsqrt(0, n)
                if n.shift(-3).real():
                    rsqrt(1, n.shift(-3))
                if n.real():
                    add_keys(n)

            loop(pool, body, LAGS)

        @block.vector
        def _(dve):
            V = nc.vector
            def statistics(which, b, src):
                for t in range(TT):
                    last = V.bn_stats(bn[which][:, t, :], src[:, t, :])
                last.then_inc(bn_done[which], 1)

            def aggregate(which, b):
                dve.wait_ge(bn_done[which], b.n + 1)
                V.memset(turnstile[which][:, :], 0.0)
                for t in range(TT):
                    last = V.bn_aggr(mv[which][:, t, :], bn[which][:, t, :])
                last.then_inc(mv_done[which], 1)

            def add_eps(which, b):
                dve.wait_ge(mv_done[which], b.n + 1)
                V.tensor_scalar(var[which][:, :], mv[which][:, :, 1], EPS, None, ALU.add).then_inc(var_done[which], 1)

            def normal(which, b, src):
                dve.wait_ge(rstd_done[which], b.n + 1)
                if b.at_least(1):
                    dve.wait_ge(xt_made[which], b.n)
                for t in range(TT):
                    last = V.tensor_scalar(xn[which][:, t, :], src[:, t, :], mv[which][:, t, 0:1], rstd[which][:, t:t + 1],
                                           ALU.subtract, ALU.mult)
                last.then_inc(xn_done[which], 1)

            def add_side(b):
                dve.wait_ge(sim_made, b.n + 1)
                dve.wait_ge(sided_b, b.n + 1)
                if b.at_least(2):
                    dve.wait_ge(pt_made, b.n - 1)
                V.scalar_tensor_tensor(out=att[b.c % 2][:, :, :], in0=sim_ps[:, 0:TT * J].rearrange("p (t j) -> p t j", t=TT), scalar=SC,
                                       in1=sided[b.c % 2][:, :, :], op0=ALU.mult, op1=ALU.add).then_inc(att_done, 1)
                dve.wait_ge(att_done, b.n + 1)
                if b.at_least(1):
                    dve.wait_ge(exped, b.n)
                V.tensor_reduce(negmax[:, :], att[b.c % 2][:, :, :], AX.X, ALU.max, negate=True).then_inc(max_done, 1)

            def invert(b):
                dve.wait_ge(exped, b.n + 1)
                V.reciprocal(rden[:, :], den[:, :]).then_inc(inverted, 1)

            def attended(b):
                dve.wait_ge(inverted, b.n + 1)
                dve.wait_ge(pv_made, b.n + 1)
                if b.at_least(4):
                    dve.wait_ge(res_done, b.n - 3)
                for t in range(TT):
                    last = V.scalar_tensor_tensor(out=x3[b.c % 4][:, t, :], in0=pv_ps[:, t * D:(t + 1) * D], scalar=rden[:, t:t + 1],
                                                  in1=x2[b.c % 4][:, t, :], op0=ALU.mult, op1=ALU.add)
                last.then_inc(x3_done, 1)

            def biased(b):
                dve.wait_ge(ff_made, b.n + 1)
                if b.at_least(1):
                    dve.wait_ge(res_done, b.n)
                V.tensor_tensor(pre[:, :, :], ff_ps[:, :].rearrange("p (t c) -> p t c", t=TT),
                                bias_w[:, :].unsqueeze(1).to_broadcast([P, TT, D]), ALU.add).then_inc(pre_done, 1)

            def body(n):
                b1, b2, b3, b4, b5 = (n.shift(-lag) for lag in range(1, 6))
                if b3.real():
                    invert(b3)
                if b2.real():
                    add_side(b2)
                if b1.real():
                    normal(0, b1, x2[b1.c % 4])
                if b5.real():
                    biased(b5)
                if b4.real():
                    normal(1, b4, x3[b4.c % 4])
                if b3.real():
                    attended(b3)
                if n.real():
                    dve.wait_ge(x_in[n.c % 4], 16 * (n.turn(4) + 1))
                    statistics(0, n, x2[n.c % 4])
                if not n.at_least(1):
                    dve.wait_ge(small_in, 32)
                    V.tensor_tensor(coef[:, :], betas[:, 0:1], betas[:, 1:2], ALU.add).then_inc(pre_set, 1)
                    dve.wait_ge(pre_set, 1)
                    V.tensor_tensor(coef[:, :], coef[:, :], betas[:, 2:3], ALU.subtract).then_inc(coef_set, 1)
                if b3.real():
                    dve.wait_ge(x3_done, b3.n + 1)
                    statistics(1, b3, x3[b3.c % 4])
                if n.real():
                    aggregate(0, n)
                if b3.real():
                    aggregate(1, b3)
                if n.real():
                    add_eps(0, n)
                if b3.real():
                    add_eps(1, b3)

            loop(dve, body, LAGS)


def make_identity(nc, ident):
    with nc.semaphore("identity_zero") as zeroed, nc.Block() as block:
        @block.gpsimd
        def _(pool):
            pool.memset(ident[:, :], 0.0).then_inc(zeroed, 1)
            pool.wait_ge(zeroed, 1)
            pool.affine_select(out=ident[:, :], in_=ident[:, :], compare_op=ALU.not_equal, fill=1.0, base=0,
                               pattern=[[-1, P]], channel_multiplier=1).then_inc(zeroed, 1)
            pool.wait_ge(zeroed, 2)


def rows_first(w):
    w = w.T
    return w.reshape(w.shape[0] // P, P, w.shape[1]).transpose(1, 0, 2)


def tiled(w):
    return w.reshape(w.shape[0] // P, P, w.shape[1]).transpose(1, 0, 2)


def layout(inputs):
    import numpy as np

    a = {k: np.asarray(v) for k, v in inputs.items()}
    wk, wv = a["L0_xattn_Wkv"][:INNER], a["L0_xattn_Wkv"][INNER:]
    ctx = a["ctx_1024"].transpose(0, 2, 1).reshape(B, KD, P, J).transpose(0, 2, 1, 3)
    return {
        "x": a["x"], "ctxt": ctx, "mask": a["mask_BxS2_bf1"].view(np.uint8),
        "wqt": rows_first(a["L0_xattn_Wq"]).reshape(P, -1), "wkt": rows_first(wk),
        "wvt": rows_first(wv).reshape(P, -1), "wot": rows_first(a["L0_xattn_Wout"]).reshape(P, -1),
        "bout": a["L0_xattn_b_out"], "wgt": rows_first(a["L0_ffn_Wg"]),
        "wq1": tiled(a["L1_xattn_Wq"]), "wk1": tiled(a["L1_xattn_Wk"]), "wv1t": rows_first(a["L1_xattn_Wv"]),
        "ffwt": rows_first(a["L1_ffn_weight"]), "ffa1": tiled(a["L1_ffn_aux_weight1"]), "ffa2": tiled(a["L1_ffn_aux_weight2"]),
        "we": np.stack([np.stack([rows_first(a[w][e]).reshape(P, -1) for w in ("L0_ffn_W1", "L0_ffn_W3", "L0_ffn_W2")], 1) for e in range(E)]),
        "wg": a["L0_ffn_Wg"], "fside": a["fside_BxSxS2_0"], "ffb": a["L1_ffn_bias"],
        "betas": np.stack([a["L1_xattn_beta_risk"], a["L1_xattn_beta_prio"], a["L1_xattn_beta_impl"]]),
        "bq": a["L1_xattn_bq"].reshape(KD, P).T, "bk": a["L1_xattn_bk"].reshape(KD, P).T, "bv": a["L1_xattn_bv"],
    }


def program(nc, io, out_dram):
    x1_dram = nc.dram_tensor("x1", [B * S, D], F32, kind="Internal").ap()
    xn1_dram = nc.dram_tensor("xn1", [B * S, D], F32, kind="Internal").ap()
    slots_dram = nc.dram_tensor("slot_tokens", [E, CAP], U32, kind="Internal").ap()
    with ExitStack() as ctx:
        def sb(name, shape, dt=F32):
            return ctx.enter_context(nc.sbuf_tensor(name, shape, dt))

        ident = sb("ident", [P, P])
        scores = sb("scores", [P, E, NT])
        make_identity(nc, ident)
        first_attention(nc, io, x1_dram, xn1_dram, ident, scores)
        expert_max, expert_inv = sb("expert_max", [P, E]), sb("expert_inv", [P, E])
        second = (sb("second_fold", [P, KD, D]), sb("second_keys", [P, B * KD, J]), sb("second_bias", [P, B, J]),
                  sb("second_values", [J, B, D]), sb("second_ffn", [P, KD, D]))
        with ExitStack() as of_experts:
            def ring(name, shape, dt):
                return [of_experts.enter_context(nc.sbuf_tensor(f"{name}{n}", shape, dt)) for n in range(2)]

            weights = (ring("expert_raw", [P, 3, KD * HID], F32), ring("expert_up_hi", [P, 2, KD * HID], F32R),
                       ring("expert_up_lo", [P, 2, KD * HID], F32R), ring("expert_down_hi", [P, KD * HID], F32R),
                       ring("expert_down_lo", [P, KD * HID], F32R))
            slots = of_experts.enter_context(nc.sbuf_tensor("slots", [P, E, QT], U32))
            xg = ring("tokens", [P, QT, D], F32)
            route(nc, io, ident, scores, slots_dram, expert_max, expert_inv, second, weights, xn1_dram, slots, xg)
            second_sems = experts(nc, io, x1_dram, xn1_dram, slots_dram, ident, expert_max, expert_inv, weights, slots, xg, ctx)
        second_layer(nc, io, x1_dram, out_dram, ident, second, second_sems)


def kernel(**inputs):
    import numpy as np
    import concourse.bacc as bacc
    from concourse.bass_utils import run_bass_kernel_spmd

    nc = bacc.Bacc("TRN2", target_bir_lowering=False, num_devices=1)
    arrays, io = {}, {}
    for name, a in layout(inputs).items():
        a = np.ascontiguousarray(a)
        arrays[f"in_{name}"] = a
        io[name] = nc.dram_tensor(f"in_{name}", a.shape, mybir.dt.from_np(a.dtype), kind="ExternalInput").ap()
    out_dram = nc.dram_tensor("out", [B, S, D], F32, kind="ExternalOutput").ap()
    program(nc, io, out_dram)
    result = run_bass_kernel_spmd(nc, [arrays], core_ids=[0])
    return result.results[0]["out"]
```
